# Optimizing a Trainium2 kernel written in Bass

```python
import numpy as np
import jax
import jax.numpy as jnp

def _softmax(x, axis=-1):
    return jax.nn.softmax(x, axis=axis)

def _gelu(x):
    return jax.nn.gelu(x, approximate=True)

def _silu(x):
    return jax.nn.silu(x)

def _sigmoid(x):
    return jax.nn.sigmoid(x)

def _layernorm(x, axis=-1, eps=1e-05):
    m = jnp.mean(x, axis=axis, keepdims=True)
    v = jnp.var(x, axis=axis, keepdims=True)
    return (x - m) / jnp.sqrt(v + eps)

def _scatter_add(tgt, idx, src, axis=0):
    return tgt.at[idx].add(src)

def _segment_sum(src, seg, n):
    return jax.ops.segment_sum(src, seg, n)
kernel_name = 'mk_decoder_preln_d1_seqx_r4_a7e439'

def setup_inputs(seed: int=0):
    np.random.seed(seed)
    _w = jnp.asarray

    def _rec_inputs():
        import jax
        import jax.numpy as jnp
        _rk = jax.random.key(seed)
        x = -0.000125 + 0.9999 * jax.random.normal(jax.random.fold_in(_rk, 1), (4, 512, 512), jnp.float32)
        _lenS = 512 - jax.random.randint(jax.random.fold_in(_rk, 7), (4,), 0, max(1, 512 // 4) + 1, jnp.int32)
        _lenS2 = 512 - jax.random.randint(jax.random.fold_in(_rk, 8), (4,), 0, max(1, 512 // 4) + 1, jnp.int32)
        itok_BxS_13_99985 = jax.random.randint(jax.random.fold_in(_rk, 11), (4, 512), 13, 99986, jnp.int32)
        _ctx_2048P = jax.random.normal(jax.random.fold_in(_rk, 12), (4, 16, 512), jnp.float32)
        _ctx_2048c = jax.random.dirichlet(jax.random.fold_in(_rk, 512), 0.3 * jnp.ones((16,), jnp.float32), (4, 512))
        _ctx_2048t = jnp.einsum('bsk,bkd->bsd', _ctx_2048c, _ctx_2048P)
        _ctx_2048t = _ctx_2048t * jax.lax.rsqrt(jnp.mean(jnp.square(_ctx_2048t)) + 1e-12) * 0.953939
        ctx_2048 = 6.82029e-06 + 0.0200006 * (_ctx_2048t + 0.3 * jax.random.normal(jax.random.fold_in(_rk, 612), (4, 512, 512), jnp.float32))
        return (x, itok_BxS_13_99985, ctx_2048)
    x, itok_BxS_13_99985, ctx_2048 = _rec_inputs()

    def _L0_attn_setup():
        import jax, jax.numpy as jnp
        import numpy as np
        B, N, E = (4, 1024, 512)
        H_DIM = 512
        HEADS = 16
        DH = H_DIM // HEADS
        LN_EPS = 1e-05

        def _heads(t):
            b, n, _ = t.shape
            return t.reshape(b, n, HEADS, DH).transpose(0, 2, 1, 3)

        def _layernorm(x, g, b):
            mu = jnp.mean(x, axis=-1, keepdims=True)
            var = jnp.mean(jnp.square(x - mu), axis=-1, keepdims=True)
            return (x - mu) * jax.lax.rsqrt(var + LN_EPS) * g + b
        key = jax.random.key(seed)
        ks = jax.random.split(key, 10)
        s = 1.0 / np.sqrt(E)
        so = 1.0 / np.sqrt(H_DIM)
        return {'x': jax.random.normal(ks[0], (B, N, E), jnp.float32), 'Wqk': jax.random.normal(ks[1], (E, H_DIM), jnp.float32) * s, 'bqk': jnp.zeros((H_DIM,), jnp.float32), 'Wv': jax.random.normal(ks[2], (E, H_DIM), jnp.float32) * s, 'bv': jnp.zeros((H_DIM,), jnp.float32), 'Wu': jax.random.normal(ks[3], (E, H_DIM), jnp.float32) * s, 'bu': jnp.zeros((H_DIM,), jnp.float32), 'Wo': jax.random.normal(ks[4], (H_DIM, E), jnp.float32) * so, 'bo': jnp.zeros((E,), jnp.float32), 'ln_g': jnp.ones((H_DIM,), jnp.float32), 'ln_b': jnp.zeros((H_DIM,), jnp.float32)}
    _L0_attn_all = _L0_attn_setup()
    _L0_attn_in = {k: v for k, v in _L0_attn_all.items() if k in ('Wqk', 'bqk', 'Wv', 'bv', 'Wu', 'bu', 'Wo', 'bo', 'ln_g', 'ln_b')}
    del _L0_attn_all

    def _L0_xattn_setup():
        import jax, jax.numpy as jnp
        import numpy as np
        B, S, D = (4, 1024, 512)
        E = 4
        F = 2048 // E
        VOCAB = 25000
        key = jax.random.key(seed)
        k1, k2, k3, k4, k5 = jax.random.split(key, 5)
        hidden_states = jax.random.normal(k1, (B, S, D), dtype=jnp.float32)
        token_ids = jax.random.randint(k2, (B, S), 0, VOCAB, dtype=jnp.int64)
        Wg = jax.random.normal(k3, (E, F, D), dtype=jnp.float32) * 0.02
        Wu = jax.random.normal(k4, (E, F, D), dtype=jnp.float32) * 0.02
        Wd = jax.random.normal(k5, (E, D, F), dtype=jnp.float32) * 0.02
        return {'hidden_states': hidden_states, 'token_ids': token_ids, 'Wg': Wg, 'Wu': Wu, 'Wd': Wd}
    _L0_xattn_all = _L0_xattn_setup()
    _L0_xattn_in = {k: v for k, v in _L0_xattn_all.items() if k in ()}
    del _L0_xattn_all

    def _L0_ffn_setup():
        import jax, jax.numpy as jnp
        import numpy as np
        D_MODEL = 512
        D_EXPERT = 2048
        EPS = 1e-08

        def ternary_quant(w):
            scale = jnp.mean(jnp.abs(w)) + EPS
            q = jnp.clip(jnp.round(w / scale), -1.0, 1.0) * scale
            return w + jax.lax.stop_gradient(q - w)
        key = jax.random.key(seed)
        k_x, k_up, k_gate, k_down = jax.random.split(key, 4)
        std_in = 1.0 / np.sqrt(D_MODEL)
        std_exp = 1.0 / np.sqrt(D_EXPERT)
        return {'x': jax.random.normal(k_x, (4, 512, D_MODEL), dtype=jnp.float32), 'W_up': jax.random.normal(k_up, (D_EXPERT, D_MODEL), dtype=jnp.float32) * std_in, 'W_gate': jax.random.normal(k_gate, (D_EXPERT, D_MODEL), dtype=jnp.float32) * std_in, 'W_down': jax.random.normal(k_down, (D_MODEL, D_EXPERT), dtype=jnp.float32) * std_exp}
    _L0_ffn_all = _L0_ffn_setup()
    _L0_ffn_in = {k: v for k, v in _L0_ffn_all.items() if k in ('W_up', 'W_gate', 'W_down')}
    del _L0_ffn_all
    return {'x': x, 'itok_BxS_13_99985': itok_BxS_13_99985, 'ctx_2048': ctx_2048, 'L0_attn_Wqk': _L0_attn_in['Wqk'], 'L0_attn_bqk': _L0_attn_in['bqk'], 'L0_attn_Wv': _L0_attn_in['Wv'], 'L0_attn_bv': _L0_attn_in['bv'], 'L0_attn_Wu': _L0_attn_in['Wu'], 'L0_attn_bu': _L0_attn_in['bu'], 'L0_attn_Wo': _L0_attn_in['Wo'], 'L0_attn_bo': _L0_attn_in['bo'], 'L0_attn_ln_g': _L0_attn_in['ln_g'], 'L0_attn_ln_b': _L0_attn_in['ln_b'], 'L0_ffn_W_up': _L0_ffn_in['W_up'], 'L0_ffn_W_gate': _L0_ffn_in['W_gate'], 'L0_ffn_W_down': _L0_ffn_in['W_down']}

def reference(x, itok_BxS_13_99985, ctx_2048, L0_attn_Wqk, L0_attn_bqk, L0_attn_Wv, L0_attn_bv, L0_attn_Wu, L0_attn_bu, L0_attn_Wo, L0_attn_bo, L0_attn_ln_g, L0_attn_ln_b, L0_ffn_W_up, L0_ffn_W_gate, L0_ffn_W_down):
    import jax
    import jax.numpy as jnp

    def _L0_attn_ref(x, Wqk, bqk, Wv, bv, Wu, bu, Wo, bo, ln_g, ln_b):
        import jax, jax.numpy as jnp
        import numpy as np
        B, N, E = (4, 1024, 512)
        H_DIM = 512
        HEADS = 16
        DH = H_DIM // HEADS
        LN_EPS = 1e-05

        def _heads(t):
            b, n, _ = t.shape
            return t.reshape(b, n, HEADS, DH).transpose(0, 2, 1, 3)

        def _layernorm(x, g, b):
            mu = jnp.mean(x, axis=-1, keepdims=True)
            var = jnp.mean(jnp.square(x - mu), axis=-1, keepdims=True)
            return (x - mu) * jax.lax.rsqrt(var + LN_EPS) * g + b
        q = x @ Wqk + bqk
        k = x @ Wqk + bqk
        v = jax.nn.silu(x @ Wv + bv)
        u = jax.nn.silu(x @ Wu + bu)
        q = jax.nn.elu(_heads(q))
        kh = jax.nn.elu(_heads(k))
        vh = _heads(v)
        kv = jnp.einsum('bhnd,bhne->bhde', kh, vh)
        out = jnp.einsum('bhnd,bhde->bhne', q, kv)
        out = out.transpose(0, 2, 1, 3).reshape(x.shape[0], x.shape[1], H_DIM)
        out = _layernorm(out, ln_g, ln_b)
        out = u * out
        return out @ Wo + bo

    def _L0_xattn_ref(hidden_states, token_ids, Wg, Wu, Wd):
        import jax, jax.numpy as jnp
        import numpy as np
        B, S, D = (4, 1024, 512)
        E = 4
        F = 2048 // E
        VOCAB = 25000
        tokens_per_expert = VOCAB // E
        tid = jnp.clip(token_ids, 0, VOCAB - 1)
        expert_ids = jnp.minimum(tid // tokens_per_expert, E - 1)
        out = jnp.zeros_like(hidden_states)
        for e in range(E):
            g = jax.nn.silu(jnp.einsum('bsd,fd->bsf', hidden_states, Wg[e]))
            u = jnp.einsum('bsd,fd->bsf', hidden_states, Wu[e])
            y = jnp.einsum('bsf,df->bsd', g * u, Wd[e])
            out = jnp.where((expert_ids == e)[..., None], y, out)
        return out

    def _L0_ffn_ref(x, W_up, W_gate, W_down):
        import jax, jax.numpy as jnp
        import numpy as np
        D_MODEL = 512
        D_EXPERT = 2048
        EPS = 1e-08

        def ternary_quant(w):
            scale = jnp.mean(jnp.abs(w)) + EPS
            q = jnp.clip(jnp.round(w / scale), -1.0, 1.0) * scale
            return w + jax.lax.stop_gradient(q - w)
        wu = ternary_quant(W_up)
        wg = ternary_quant(W_gate)
        wd = ternary_quant(W_down)
        up = jnp.einsum('bsd,ed->bse', x, wu)
        gate = jnp.einsum('bsd,ed->bse', x, wg)
        hidden = jax.nn.silu(up) * gate
        return jnp.einsum('bse,de->bsd', hidden, wd)
    x = x + _L0_attn_ref(_layernorm(x, axis=-1), L0_attn_Wqk, L0_attn_bqk, L0_attn_Wv, L0_attn_bv, L0_attn_Wu, L0_attn_bu, L0_attn_Wo, L0_attn_bo, L0_attn_ln_g, L0_attn_ln_b)
    x = x + _L0_xattn_ref(_layernorm(x, axis=-1), itok_BxS_13_99985, ctx_2048, ctx_2048, ctx_2048)
    x = x + _L0_ffn_ref(_layernorm(x, axis=-1), L0_ffn_W_up, L0_ffn_W_gate, L0_ffn_W_down)
    return x

_drawn_inputs = setup_inputs


def setup_inputs(seed=0):
    import zlib

    import numpy as np

    out = dict(_drawn_inputs(seed))
    spreads = {'L0_attn_bqk': (0.0, 0.1),
     'L0_attn_bv': (0.0, 0.1),
     'L0_attn_bu': (0.0, 0.1),
     'L0_attn_bo': (0.0, 0.1),
     'L0_attn_ln_g': (1.0, 0.2),
     'L0_attn_ln_b': (0.0, 0.1)}
    factors = {}
    for name, (base, spread) in spreads.items():
        noise = np.random.default_rng([zlib.crc32(name.encode()), seed]).standard_normal(out[name].shape)
        drawn = base * np.exp(spread * noise) if base else spread * noise
        out[name] = jnp.asarray(drawn.astype(out[name].dtype))
    for name, factor in factors.items():
        out[name] = (out[name] * factor).astype(out[name].dtype)
    return out
```

```python
from contextlib import ExitStack

import numpy as np

import concourse.bass as bass
from concourse import mybir

ALU = mybir.AluOpType
ACT = mybir.ActivationFunctionType
AX = mybir.AxisListType
F32 = mybir.dt.float32
F16 = mybir.dt.float16
BF16 = mybir.dt.bfloat16
I32 = mybir.dt.int32

P = 128
B, S, D = 4, 512, 512
FF = 2048
K = D // P
T = S // P
NT = B * T
HD = 32
E = 4
VOCAB = 25000
SLOTS = NT + E - 1
C = FF // P
CTX_SCALE = 256.0
HID_SCALE = 8.0
LN_EPS = 1e-5
Q_EPS = 1e-8
PARTS = ((0, 0), (1, 0), (0, 1))


def decoder(nc, x, itok, ctx_w, Wqk, bqk, Wv, bv, Wu, bu, Wo, bo, ln_g, ln_b, W_up, W_gate, W_down, out):
    es = ExitStack()

    def sb(name, shape, dt=F32):
        return es.enter_context(nc.sbuf_tensor(name, shape, dt))

    def sem(name):
        return es.enter_context(nc.semaphore(name))

    x_v = x.rearrange("b (t p) d -> p (b t) d", p=P)
    out_v = out.rearrange("b (t p) d -> p (b t) d", p=P)
    tok_v = itok.rearrange("b (t p) -> p (b t)", p=P)
    ctx_v = ctx_w.rearrange("e (r p) d -> p e r d", p=P)
    att_v = [w.rearrange("(k p) n -> p k n", p=P) for w in (Wqk, Wv, Wu, Wo)]
    unit_v = [W_up.rearrange("(g r p) d -> p g r d", r=T, p=P),
              W_gate.rearrange("(g r p) d -> p g r d", r=T, p=P),
              W_down.rearrange("(g p) (r d) -> p g r d", p=P, r=T)]
    column = lambda v: v.rearrange("(k p) -> p k", p=P)
    xs_dram = nc.dram_tensor("sorted_tokens", ((SLOTS + 1) * P, D), F32, kind="Internal").ap()
    ys_dram = nc.dram_tensor("sorted_outputs", (SLOTS * P, D), F32, kind="Internal").ap()
    xs_v = xs_dram.rearrange("(c p) d -> p c d", p=P)
    ys_v = ys_dram.rearrange("(c p) d -> p c d", p=P)

    resid = sb("resid", [P, NT, D])
    w_att = sb("w_att", [P, 4, 2, K, D], F16)
    w_moe = sb("w_moe", [P, E, 2, K, D], F16)
    region = sb("region", [P, 6, T, D])
    stage = sb("stage", [P, 2, T, D])
    nrm = sb("nrm", [P, T, D])
    n2 = sb("n2", [P, T, D])
    tmp = sb("tmp", [P, 2, D])
    tmpA = sb("tmpA", [P, 2, D])
    a32 = sb("a32", [P, 2, D])
    kvm = sb("kvm", [P, K, P])
    xT = sb("xT", [P, 2, K, S], F16)
    bv_bc = sb("bv_bc", [P, D])
    bo_bc = sb("bo_bc", [P, D])
    head_mask = sb("head_mask", [P, K, P])
    cols = sb("cols", [P, 4, K])
    ident = sb("ident", [P, P])
    ident_b = sb("ident_b", [P, P], BF16)
    ones = sb("ones", [P, P])
    tri = sb("tri", [P, P])
    halfs = sb("halfs", [P, T])
    st = [sb(f"st{i}", [P, T, 6]) for i in range(3)]
    mv = [sb(f"mv{i}", [P, T, 2]) for i in range(3)]
    ve = [sb(f"ve{i}", [P, T]) for i in range(3)]
    rs = [sb(f"rs{i}", [P, T]) for i in range(3)]
    absacc = sb("absacc", [P, 3, B])
    abssum = sb("abssum", [P, 3])
    qs = sb("qs", [P, 3])
    thr = sb("thr", [P, 2, 3])
    hk = sb("hk", [P, 2])
    tok = sb("tok", [P, NT], I32)
    tokf = sb("tokf", [P, NT])
    pad_i = sb("pad_i", [P, 2, E], I32)
    pad_f = sb("pad_f", [P, E])
    base = sb("base", [P, E])
    pos_f = sb("pos_f", [P, NT])
    pos = sb("pos", [P, NT + 1], I32)
    pos_now = sb("pos_now", [P, T], I32)
    starts_i = sb("starts_i", [1, SLOTS], I32)
    starts = sb("starts", [1, SLOTS])
    te_f = sb("te_f", [1, E, SLOTS])
    tile_expert = sb("tile_expert", [1, SLOTS], I32)

    rt = region[:, 5, 0, 0:(3 * E + 1 + E) * NT].rearrange("p (e c) -> p e c", c=NT)
    ge, member, before = rt[:, 0:E + 1], rt[:, E + 1:2 * E + 1], rt[:, 2 * E + 1:3 * E + 1]
    scan = region[:, 5, 1, 0:2 * E * NT].rearrange("p (i e c) -> p i e c", i=2, e=E)
    qT, kk, vv, uT, on = [region[:, i] for i in range(5)]
    aT = region[:, 5].rearrange("p a b -> p (a b)").bitcast(F16).rearrange("p (h k s) -> p h k s", h=2, k=K)
    tern = [region[:, 2 * i:2 * i + 2].rearrange("p a b c -> p (a b c)").bitcast(BF16)
            .rearrange("p (c n) -> p c n", c=C) for i in range(3)]
    signs = w_att[:].rearrange("p a b c d -> p (a b c d)")[:, 0:6 * FF].bitcast(BF16).rearrange(
        "p (j s r d) -> p j s r d", j=3, s=2, r=T)
    x3T = w_att
    att_slot = [stage[:, 0], stage[:, 1], on, n2[:, :, :]]
    out_slot = [stage[:, 0, t] for t in range(T)]
    unit_slot = [stage[:, 0], stage[:, 1], nrm[:, :, :]]
    xs_slot = [n2[:, i] for i in range(3)]
    ys_slot = [n2[:, 3], a32[:, 0], a32[:, 1]]
    sil, h32 = tmp[:, 0], tmp[:, 1]
    tA = tmpA[:].rearrange("p a b -> p (a b)").bitcast(F16).rearrange("p (i h n) -> p i h n", i=2, h=2)
    xsT, hT = tA[:, 0], tA[:, 1]
    hid = tA

    ps = [es.enter_context(nc.psum_tensor(f"bank{i}", [P, 512], F32)) for i in range(8)]
    acc, tr, kv_ps, o_ps, prep = ps[0:2], ps[2:4], ps[4], ps[5:7], ps[7]
    z_ps, y_ps, tx_ps, th_ps, q_ps = ps[0], ps[1], ps[2], ps[3], ps[4:8]
    ffy_ps, up_ps, gate_ps, t3_ps = ps[0:4], ps[4], ps[5], ps[6]

    names = """x_first x_rest cols_in rows_in tok_in att_in0 att_in1 att_in2 att_in3 stage_in0 stage_in1
        zeroed scattered xs_in0 xs_in1 xs_in2 unit_in0 unit_in1 unit_in2 ys_out0 ys_out1 ys_out2 y_in y_in_first
        out_done0 out_done1 out_done2 out_done3
        ident_made pool_const zero_src starts_made bias_added rs1 rs_o rs2 rs3 rs3_first
        w_hi w_lo ctx_mm ctx_hi ctx_lo abs_done abs_mm scale_step
        route_step route_mm route_read route_ready
        x_stat x_aggr x_norm t1_mm x_hi x_lo
        q_mm q_exp q_clip q_elu tn_mm n_aff a_mul a_hi a_lo v_mm v_bias v_act wo_mm x1_done
        x2_stat x2_aggr x2_norm pos_copied tk_mm k_copy u_mm u_act kv_mm kv_evac o_mm o_copy o_stat o_aggr o_norm
        tx_mm xs_hi xs_lo z_mm z_act h_mul th_mm h_hi h_lo y_mm y_evac sign_a sign_b unit_mm unit_copy
        y_added x3_stat x3_aggr x3_norm t3_mm x3_hi x3_lo pos3_copied
        up_mm gate_mm up_act hid_mul hid_hi hid_lo down_mm out_made""".split()
    s = {n: sem(n) for n in names}

    def wait_apart(eng, name, value):
        if not isinstance(value, int):
            eng.lower_val(value)
        eng.wait_ge(s["zero_src"], 1)
        eng.wait_ge(s[name], value)

    block = es.enter_context(nc.Block())

    @block.sync
    def _(sp):
        sp.dma_start(resid[:, 0:T], x_v[:, 0:T]).then_inc(s["x_first"], 16)
        sp.dma_start(att_slot[0], att_v[0]).then_inc(s["att_in0"], 16)
        for i, v in enumerate((bqk, bu, ln_g, ln_b)):
            sp.dma_start(cols[:, i], column(v), allow_slow_non_contiguous=True).then_inc(s["cols_in"], 16)
        sp.dma_start(tok[:, :], tok_v, allow_slow_non_contiguous=True).then_inc(s["tok_in"], 16)
        for m in (1, 2, 3):
            sp.dma_start(att_slot[m], att_v[m]).then_inc(s[f"att_in{m}"], 16)
        sp.dma_start(bv_bc[:, :], bv.partition_broadcast(P)).then_inc(s["rows_in"], 16)
        sp.dma_start(bo_bc[:, :], bo.partition_broadcast(P)).then_inc(s["rows_in"], 16)
        sp.dma_start(resid[:, T:NT], x_v[:, T:NT]).then_inc(s["x_rest"], 16)

        def expert_weights(b):
            sp.dma_start(stage[:, 0], ctx_v[:, bass.ds(b, 1)].rearrange("p a r d -> p (a r) d")).then_inc(
                s["stage_in0"], 16)

        def summed_unit(b, j, slot):
            sp.dma_start(stage[:, slot], unit_v[j][:, bass.ds(b, 1)].rearrange("p a r d -> p (a r) d")).then_inc(
                s[f"stage_in{slot}"], 16)

        def weights(b, first):
            if first:
                sp.wait_ge(s["w_lo"], 1)
                expert_weights(b)
                sp.wait_ge(s["w_lo"], 2)
                summed_unit(b, 0, 1)
                sp.wait_ge(s["zero_src"], 1)
                with sp.Fori(0, (SLOTS + 1) // 2) as i:
                    sp.dma_start(xs_v[:, bass.ds(2 * i, 2)], a32[:, :, :]).then_inc(s["zeroed"], 16)
            else:
                sp.wait_ge(s["abs_done"], 3 * b - 1)
                expert_weights(b)
                sp.wait_ge(s["abs_done"], 3 * b)
                summed_unit(b, 0, 1)
            sp.wait_ge(s["ctx_mm"], 4 * b + 4)
            summed_unit(b, 1, 0)
            sp.wait_ge(s["abs_done"], 3 * b + 1)
            summed_unit(b, 2, 1)

        weights(0, True)
        with sp.Fori(1, B) as b:
            weights(b, False)

        def unit(g, j):
            sp.dma_start(unit_slot[j], unit_v[j][:, bass.ds(g, 1)].rearrange("p a r d -> p (a r) d")).then_inc(
                s[f"unit_in{j}"], 16)

        def sorted_tile(i, slot):
            sp.dma_start(xs_slot[slot], xs_v[:, bass.ds(i, 1)].rearrange("p a d -> p (a d)")).then_inc(
                s[f"xs_in{slot}"], 16)

        sp.wait_ge(s["abs_done"], 3 * B)
        sp.wait_ge(s["t1_mm"], T * (B + 1))
        for j in range(3):
            unit(0, j)
        for j in range(3):
            sp.wait_ge(s["sign_b"], j + 1)
            unit(1, j)
        sp.wait_ge(s["scattered"], 16 * NT)
        for i in range(3):
            sorted_tile(i, i)
        for g in (2, 3):
            for j in range(3):
                sp.wait_ge(s["sign_b"], 3 * (g - 1) + j + 1)
                unit(g, j)
                sp.wait_ge(s["tx_mm"], 3 * (g - 2) + j + 1)
                sorted_tile(3 * (g - 1) + j, j)
        with sp.Fori(2, 5) as g:
            for j in range(3):
                sp.wait_ge(s["tx_mm"], 3 * g + j + 1)
                sorted_tile(3 * g + j + 3, j)
        for i in (18, 19):
            sp.wait_ge(s["tx_mm"], i - 2)
            sorted_tile(i, i % 3)

        with sp.Fori(0, B) as b:
            for t in range(T):
                sp.wait_ge(s["out_made"], T * b + t + 1)
                sp.dma_start(out_v[:, bass.ds(T * b + t, 1)].rearrange("p a d -> p (a d)"), out_slot[t]).then_inc(
                    s[f"out_done{t}"], 16)
        for t in range(T):
            sp.wait_ge(s[f"out_done{t}"], 16 * B)

    @block.gpsimd
    def _(pool):
        pool.memset(ones[:, :], 1.0).then_inc(s["pool_const"], 1)
        pool.memset(halfs[:, :], -0.5).then_inc(s["pool_const"], 1)
        pool.wait_ge(s["pool_const"], 2)
        pool.affine_select(out=ident[:, :], in_=ones[:, :], compare_op=ALU.is_equal, fill=0.0, base=0,
                           pattern=[[-1, P]], channel_multiplier=1).then_inc(s["ident_made"], 1)
        pool.affine_select(out=tri[:, :], in_=ones[:, :], compare_op=ALU.is_gt, fill=0.0, base=0,
                           pattern=[[1, P]], channel_multiplier=-1).then_inc(s["pool_const"], 1)
        pool.memset(a32[:, :, :], 0.0).then_inc(s["zero_src"], 1)

        def late_constants():
            pool.memset(head_mask[:, :, :], 1.0).then_inc(s["pool_const"], 1)
            pool.wait_ge(s["pool_const"], 4)
            hm = head_mask[:].rearrange("p k (j e) -> p k j e", e=HD)
            pool.affine_select(out=hm, in_=hm, compare_op=ALU.is_ge, fill=0.0, base=0,
                               pattern=[[0, K], [-HD, P // HD], [0, HD]], channel_multiplier=1).then_inc(s["pool_const"], 1)
            pool.wait_ge(s["pool_const"], 5)
            pool.affine_select(out=hm, in_=hm, compare_op=ALU.is_ge, fill=0.0, base=HD - 1,
                               pattern=[[0, K], [HD, P // HD], [0, HD]], channel_multiplier=-1).then_inc(s["pool_const"], 1)
            pool.tensor_copy(ident_b[:, :], ident[:, :]).then_inc(s["pool_const"], 1)
            pool.iota(starts_i[:, :], pattern=[[P, SLOTS]], base=0, channel_multiplier=0).then_inc(s["starts_made"], 1)

        def rsqrt(i, aggr, n, done, k, wait):
            wait_apart(pool, aggr, wait)
            pool.tensor_scalar(ve[i][:, 0:n], mv[i][:, 0:n, 1], LN_EPS, 0.0, ALU.add, ALU.add).then_inc(s[done], 1)
            pool.wait_ge(s[done], 2 * k + 1)
            pool.tensor_tensor(rs[i][:, 0:n], ve[i][:, 0:n], halfs[:, 0:n], ALU.pow).then_inc(s[done], 1)

        def project(b):
            rsqrt(2, "x2_aggr", T, "rs2", b, T * b + T)
            for t in range(T):
                wait_apart(pool, "x2_norm", T * b + t + 1)
                pool.indirect_dma_start(xs_dram, bass.IndirectOffsetOnAxis(ap=pos_now[:, t:t + 1], axis=0),
                                        n2[:, t], None).then_inc(s["scattered"], 16)

        def batch(b, first):
            pool.wait_ge(s["x_norm"], T * b + T)
            for t in range(T):
                xt = resid[:, bass.ds(T * b + t, 1)].rearrange("p a d -> p (a d)")
                pool.tensor_tensor(xt, xt, bo_bc[:, :], ALU.add).then_inc(s["bias_added"], 1)
            if not first:
                pool.wait_ge(s["pos_copied"], b)
                project(b - 1)
            rsqrt(0, "x_aggr", T, "rs1", b + 1, T * b + 2 * T)
            rsqrt(1, "o_aggr", T, "rs_o", b, T * b + T)

        rsqrt(0, "x_aggr", T, "rs1", 0, T)
        late_constants()
        pool.wait_ge(s["rows_in"], 32)
        batch(0, True)
        pool.wait_ge(s["zeroed"], 16 * ((SLOTS + 1) // 2))
        with pool.Fori(1, B) as b:
            batch(b, False)
        pool.wait_ge(s["pos_copied"], B)
        project(B - 1)

        def store(i, slot, j):
            pool.wait_ge(s["y_evac"], j)
            pool.dma_start(ys_v[:, bass.ds(i, 1)].rearrange("p a d -> p (a d)"), ys_slot[slot]).then_inc(
                s[f"ys_out{slot}"], 16)

        with pool.Fori(0, 6) as g:
            for j in range(3):
                store(3 * g + j, j, 3 * g + j + 1)
        store(SLOTS - 1, 0, SLOTS)

        for slot, n in enumerate((7, 6, 6)):
            pool.wait_ge(s[f"ys_out{slot}"], 16 * n)

        for t in range(T):
            pool.wait_ge(s["pos3_copied"], 1)
            pool.indirect_dma_start(n2[:, t], None, ys_dram,
                                    bass.IndirectOffsetOnAxis(ap=pos_now[:, t:t + 1], axis=0)).then_inc(s["y_in_first"], 16)
        rsqrt(0, "x3_aggr", T, "rs3_first", 0, T)
        with pool.Fori(T, NT) as i:
            wait_apart(pool, "pos3_copied", i - T + 2)
            pool.indirect_dma_start(n2[:, 0], None, ys_dram,
                                    bass.IndirectOffsetOnAxis(ap=pos_now[:, 0:1], axis=0)).then_inc(s["y_in"], 16)
            rsqrt(0, "x3_aggr", 1, "rs3", i - T, i + 1)

    @block.scalar
    def _(act):
        def first_norm(b1):
            for t in range(T):
                act.wait_ge(s["t1_mm"], T * b1 + t + 1)
                act.activation(xT[:, 0, :, t * P:(t + 1) * P], tr[t % 2].rearrange("p (k s) -> p k s", k=K),
                               ACT.Copy).then_inc(s["x_hi"], 1)

        def split(m):
            act.wait_ge(s[f"att_in{m}"], 16)
            act.activation(w_att[:, m, 0], att_slot[m], ACT.Copy).then_inc(s["w_hi"], 1)

        def ctx_hi(b, k):
            act.wait_ge(s["ctx_mm"], 4 * b + k + 1)
            act.activation(w_moe[:, bass.ds(b, 1), 0, k].rearrange("p a d -> p (a d)"), prep[:, :], ACT.Copy,
                           scale=CTX_SCALE).then_inc(s["ctx_hi"], 1)

        def affine(b, k):
            act.wait_ge(s["tn_mm"], K * b + k + 1)
            act.wait_ge(s["a_mul"], K * b + (k - 1 if k >= 2 else 0))
            act.activation(tmpA[:, k % 2], tr[k % 2][:, :], ACT.Identity, bias=cols[:, 3, k:k + 1],
                           scale=cols[:, 2, k:k + 1]).then_inc(s["n_aff"], 1)

        def gated_hi(b, k):
            act.wait_ge(s["a_mul"], K * b + k + 1)
            act.wait_ge(s["wo_mm"], T * b)
            act.activation(aT[:, 0, k], a32[:, k % 2], ACT.Copy).then_inc(s["a_hi"], 1)

        def v_act(b, t):
            act.wait_ge(s["v_bias"], T * b + t + 1)
            act.activation(vv[:, t], vv[:, t], ACT.Silu).then_inc(s["v_act"], 1)

        def magnitudes(b, j):
            slot, n = ((1, 1), (0, 2), (1, 2))[j]
            act.wait_ge(s[f"stage_in{slot}"], 32 * b + 16 * n)
            act.activation(stage[:, slot], stage[:, slot], ACT.Abs,
                           accum_out=absacc[:, j, bass.ds(b, 1)]).then_inc(s["abs_done"], 1)

        def batch(b, first):
            for m in range(K):
                act.wait_ge(s["q_mm"], K * b + m + 1)
                if not first or m >= 2:
                    act.wait_ge(s["q_elu"], K * b + m - 1)
                act.activation(tmp[:, m % 2], acc[m % 2][:, :], ACT.Exp, bias=cols[:, 0, m:m + 1]).then_inc(s["q_exp"], 1)
            if first:
                split(2)
                for t in range(T):
                    v_act(b, t)
                split(3)
            else:
                ctx_hi(b, 0)
                affine(b - 1, 0)
                affine(b - 1, 1)
                gated_hi(b - 1, 0)
                affine(b - 1, 2)
                gated_hi(b - 1, 1)
                v_act(b, 0)
                affine(b - 1, 3)
                gated_hi(b - 1, 2)
                v_act(b, 1)
                gated_hi(b - 1, 3)
                v_act(b, 2)
                v_act(b, 3)
                ctx_hi(b, 1)
                ctx_hi(b, 2)
            act.wait_ge(s["kv_mm"], b)
            for t in range(T):
                act.wait_ge(s["tk_mm"], T * b + t + 1)
                act.activation(kk[:, t], tr[t % 2][:, :], ACT.Copy).then_inc(s["k_copy"], 1)
            ctx_hi(b, 0 if first else 3)
            magnitudes(b, 0)
            act.wait_ge(s["a_mul"], K * b)
            for m in range(K):
                act.wait_ge(s["u_mm"], K * b + m + 1)
                act.activation(uT[:, m], acc[m % 2][:, :], ACT.Silu, bias=cols[:, 1, m:m + 1]).then_inc(s["u_act"], 1)
                if first and m < 3:
                    ctx_hi(b, m + 1)
                if m == 2:
                    magnitudes(b, 1)
            first_norm(b + 1)
            act.wait_ge(s["tn_mm"], K * b)
            for t in range(T):
                act.wait_ge(s["o_mm"], T * b + t + 1)
                act.activation(on[:, t], o_ps[t % 2][:, :], ACT.Copy).then_inc(s["o_copy"], 1)
            magnitudes(b, 2)

        def unit_copies(g, j):
            for r in range(T):
                act.wait_ge(s["unit_mm"], T * (3 * g + j) + r + 1)
                if j < 2:
                    dst, src = tern[j][:, T * g + r], q_ps[r][:, :]
                else:
                    dst, src = tern[j][:, T * r:T * r + T, P * g:P * g + P], q_ps[r].rearrange("p (c d) -> p c d", c=T)
                act.activation(dst, src, ACT.Copy).then_inc(s["unit_copy"], 1)

        split(0)
        first_norm(0)
        split(1)
        act.wait_ge(s["cols_in"], 64)
        batch(0, True)
        with act.Fori(1, B) as b:
            batch(b, False)
        unit_copies(0, 0)
        affine(B - 1, 0)
        for k in range(1, K):
            affine(B - 1, k)
            gated_hi(B - 1, k - 1)
        gated_hi(B - 1, K - 1)
        unit_copies(0, 1)
        act.wait_ge(s["wo_mm"], T * B)
        for g, j in ((0, 2), (1, 0), (1, 1), (1, 2)):
            unit_copies(g, j)

        def xs_hi(i):
            act.wait_ge(s["tx_mm"], i + 1)
            act.wait_ge(s["z_mm"], i)
            act.activation(xsT[:, 0], tx_ps[:, :], ACT.Copy).then_inc(s["xs_hi"], 1)

        def tile_step(i, quant):
            act.wait_ge(s["z_mm"], i + 1)
            act.wait_ge(s["h_mul"], i)
            act.activation(sil, z_ps[:, :], ACT.Silu, scale=1.0 / CTX_SCALE).then_inc(s["z_act"], 1)
            xs_hi(i + 1)
            act.wait_ge(s["th_mm"], i + 1)
            act.wait_ge(s["y_mm"], i)
            act.activation(hT[:, 0], th_ps[:, :], ACT.Copy).then_inc(s["h_hi"], 1)
            if quant is not None:
                unit_copies(*quant)

        xs_hi(0)
        tile_step(0, None)
        for j in range(3):
            tile_step(j + 1, (2, j))
        with act.Fori(T, SLOTS) as i:
            tile_step(i, None)
        for j in range(3):
            unit_copies(3, j)

        def x3_hi(b, t):
            act.wait_ge(s["t3_mm"], T * b + t + 1)
            act.activation(x3T[:, bass.ds(b, 1), 0, :, bass.ds(t * P, P)].rearrange("p a k s -> p (a k) s"),
                           t3_ps[:, :].rearrange("p (k s) -> p k s", k=K), ACT.Copy).then_inc(s["x3_hi"], 1)

        def group(b, t, first, nxt):
            for cc in range(4):
                cf = C * b + 4 * t + cc
                act.wait_ge(s["up_mm"], cf + 1)
                act.wait_ge(s["hid_mul"], cf)
                act.activation(sil, up_ps[:, :], ACT.Silu, scale=qs[:, 0:1]).then_inc(s["up_act"], 1)
                act.wait_ge(s["hid_mul"], cf + 1)
                if not (first and cc < 2):
                    act.wait_ge(s["down_mm"], cf - 1)
                act.activation(hid[:, cc % 2, 0], h32, ACT.Copy).then_inc(s["hid_hi"], 1)
                if nxt and cc == 3:
                    x3_hi(b + 1, t)

        for t in range(T):
            x3_hi(0, t)

        def batch3(b, first, nxt):
            group(b, 0, first, nxt)
            with act.Fori(1, T) as t:
                group(b, t, False, nxt)

        batch3(0, True, True)
        with act.Fori(1, B - 1) as b:
            batch3(b, False, True)
        batch3(B - 1, False, False)

    @block.vector
    def _(dve):
        def stats(i, src, stat, aggr, n0, wait_each=None):
            for t in range(T):
                if wait_each:
                    wait_apart(dve, wait_each, n0 + t + 1)
                dve.bn_stats(st[i][:, t], src(t)).then_inc(s[stat], 1)
            wait_apart(dve, stat, n0 + T)
            for t in range(T):
                dve.bn_aggr(mv[i][:, t], st[i][:, t]).then_inc(s[aggr], 1)

        def normalise(i, dst, src, t, done):
            dve.tensor_scalar(dst, src, mv[i][:, t, 0:1], rs[i][:, t:t + 1], ALU.subtract, ALU.mult).then_inc(s[done], 1)

        def x_tile(n):
            return resid[:, bass.ds(n, 1)].rearrange("p a d -> p (a d)")

        def first_norm_a(b1, wrap):
            n0 = T * wrap
            stats(0, lambda t: x_tile(n0 + t), "x_stat", "x_aggr", T * b1)

        def first_norm_b(b1, wrap):
            dve.wait_ge(s["rs1"], 2 * b1 + 2)
            dve.wait_ge(s["t1_mm"], T * b1)
            for t in range(T):
                normalise(0, nrm[:, t], x_tile(T * wrap + t), t, "x_norm")

        def first_norm_lo(b1):
            for t in range(T):
                dve.wait_ge(s["x_hi"], T * b1 + t + 1)
                cut = slice(t * P, (t + 1) * P)
                dve.tensor_tensor(xT[:, 1, :, cut], tr[t % 2].rearrange("p (k s) -> p k s", k=K),
                                  xT[:, 0, :, cut], ALU.subtract).then_inc(s["x_lo"], 1)

        def split(m):
            dve.wait_ge(s["w_hi"], m + 1)
            dve.tensor_tensor(w_att[:, m, 1], att_slot[m], w_att[:, m, 0], ALU.subtract).then_inc(s["w_lo"], 1)

        step = [0]

        def route(ins):
            step[0] += 1
            ins.then_inc(s["route_step"], 1)
            dve.wait_ge(s["route_step"], step[0])

        def routing_members():
            dve.wait_ge(s["tok_in"], 16)
            route(dve.tensor_copy(tokf[:, :], tok[:, :]))
            dve.memset(ge[:, 0], 1.0).then_inc(s["route_step"], 1)
            dve.memset(ge[:, E], 0.0).then_inc(s["route_step"], 1)
            for e in range(1, E):
                dve.tensor_scalar(ge[:, e], tokf[:, :], float(e * (VOCAB // E)), None, ALU.is_ge).then_inc(s["route_step"], 1)
            step[0] += E + 1
            dve.wait_ge(s["route_step"], step[0])
            route(dve.tensor_tensor(member[:, :, :], ge[:, 0:E], ge[:, 1:E + 1], ALU.subtract))

        def routing_starts():
            dve.wait_ge(s["route_mm"], 2)
            route(dve.tensor_copy(scan[:, 0], kv_ps[:, 0:E * NT].rearrange("p (e c) -> p e c", e=E)))
            dve.tensor_tensor(before[:, :, :], kv_ps[:, E * NT:2 * E * NT].rearrange("p (e c) -> p e c", e=E),
                              scan[:, 0], ALU.subtract).then_inc(s["route_read"], 1)
            dve.wait_ge(s["route_read"], 1)
            a, d = 0, 1
            while d < NT:
                dve.tensor_copy(scan[:, 1 - a, :, 0:d], scan[:, a, :, 0:d]).then_inc(s["route_step"], 1)
                step[0] += 1
                route(dve.tensor_tensor(scan[:, 1 - a, :, d:NT], scan[:, a, :, d:NT], scan[:, a, :, 0:NT - d], ALU.add))
                a, d = 1 - a, 2 * d
            count = scan[:, a, :, NT - 1]
            route(dve.tensor_scalar(pad_f[:, :], count, float(P - 1), None, ALU.add))
            route(dve.tensor_copy(pad_i[:, 0], pad_f[:, :]))
            route(dve.tensor_scalar(pad_i[:, 1], pad_i[:, 0], 7, 7, ALU.logical_shift_right, ALU.logical_shift_left))
            route(dve.tensor_copy(pad_f[:, :], pad_i[:, 1]))
            route(dve.memset(base[:, :], 0.0))
            for e in range(1, E):
                route(dve.tensor_tensor(base[:, e:e + 1], base[:, e - 1:e], pad_f[:, e - 1:e], ALU.add))
            assert d == NT and a == 0

        def routing_positions():
            a = 0
            route(dve.tensor_tensor(before[:, :, :], before[:, :, :], scan[:, a], ALU.add))
            for e in range(E):
                dve.tensor_scalar(ge[:, e], before[:, e], base[:, e:e + 1], None, ALU.add).then_inc(s["route_step"], 1)
            step[0] += E
            dve.wait_ge(s["route_step"], step[0])
            route(dve.tensor_tensor(before[:, :, :], ge[:, 0:E], member[:, :, :], ALU.mult))
            route(dve.tensor_reduce(pos_f[:, :], before[:, :, :].rearrange("p e c -> p c e"), AX.X, ALU.add))
            route(dve.memset(pos[:, NT:NT + 1], 0))
            route(dve.tensor_copy(pos[:, 0:NT], pos_f[:, :]))
            dve.wait_ge(s["starts_made"], 1)
            route(dve.tensor_copy(starts[:, :], starts_i[:, :]))
            for e in range(1, E):
                dve.tensor_scalar(te_f[:, e], starts[:, :], base[0:1, e:e + 1], None, ALU.is_ge).then_inc(s["route_step"], 1)
            step[0] += E - 1
            dve.wait_ge(s["route_step"], step[0])
            route(dve.tensor_tensor(te_f[:, 0], te_f[:, 1], te_f[:, 2], ALU.add))
            route(dve.tensor_tensor(te_f[:, 1], te_f[:, 0], te_f[:, 3], ALU.add))
            dve.tensor_copy(tile_expert[:, :], te_f[:, 1]).then_inc(s["route_ready"], 1)

        dve.wait_ge(s["x_first"], 16)
        first_norm_a(0, 0)
        first_norm_b(0, 0)
        split(0)
        first_norm_lo(0)
        split(1)
        routing_members()
        dve.wait_ge(s["cols_in"], 64)

        def gated_mul(b, k):
            if k == 0:
                dve.wait_ge(s["zeroed"], 16 * ((SLOTS + 1) // 2))
                dve.wait_ge(s["u_act"], K * b + K)
            dve.wait_ge(s["n_aff"], K * b + k + 1)
            dve.tensor_tensor(a32[:, k % 2], tmpA[:, k % 2], uT[:, k], ALU.mult).then_inc(s["a_mul"], 1)

        def gated_lo(b, k):
            dve.wait_ge(s["a_hi"], K * b + k + 1)
            dve.tensor_tensor(aT[:, 1, k], a32[:, k % 2], aT[:, 0, k], ALU.subtract).then_inc(s["a_lo"], 1)

        def v_bias(b, t):
            dve.wait_ge(s["v_mm"], T * b + t + 1)
            dve.tensor_tensor(vv[:, t], acc[t % 2][:, :], bv_bc[:, :], ALU.add).then_inc(s["v_bias"], 1)

        def head_norm(b):
            dve.wait_ge(s["rs_o"], 2 * b + 2)
            for t in range(T):
                normalise(1, on[:, t], on[:, t], t, "o_norm")

        def residual(b):
            for t in range(T):
                dve.wait_ge(s["wo_mm"], T * b + t + 1)
                dve.wait_ge(s["bias_added"], T * b + t + 1)
                dve.tensor_tensor(x_tile(T * b + t), acc[t % 2][:, :], x_tile(T * b + t), ALU.add).then_inc(s["x1_done"], 1)

        def second_stats(b):
            stats(2, lambda t: x_tile(T * b + t), "x2_stat", "x2_aggr", T * b, "x1_done")

        def second_norm(b):
            dve.wait_ge(s["rs2"], 2 * b + 2)
            dve.wait_ge(s["scattered"], 16 * T * b)
            for t in range(T):
                normalise(2, n2[:, t], x_tile(T * b + t), t, "x2_norm")

        def copy_pos(b):
            dve.wait_ge(s["scattered"], 16 * T * b)
            dve.tensor_copy(pos_now[:, :], pos[:, bass.ds(T * b, T)]).then_inc(s["pos_copied"], 1)

        def ctx_lo(b, k):
            dve.wait_ge(s["ctx_hi"], 4 * b + k + 1)
            hi = w_moe[:, bass.ds(b, 1), 0, k].rearrange("p a d -> p (a d)")
            lo = w_moe[:, bass.ds(b, 1), 1, k].rearrange("p a d -> p (a d)")
            dve.scalar_tensor_tensor(out=lo, in0=prep[:, :], scalar=CTX_SCALE, in1=hi, op0=ALU.mult,
                                     op1=ALU.subtract).then_inc(s["ctx_lo"], 1)

        def q_elu(b, m):
            dve.wait_ge(s["q_exp"], K * b + m + 1)
            dve.tensor_scalar(tmp[:, m % 2], tmp[:, m % 2], 1.0, -1.0, ALU.min, ALU.add).then_inc(s["q_clip"], 1)
            dve.wait_ge(s["q_clip"], K * b + m + 1)
            dve.scalar_tensor_tensor(out=qT[:, m], in0=acc[m % 2][:, :], scalar=cols[:, 0, m:m + 1],
                                     in1=tmp[:, m % 2], op0=ALU.add, op1=ALU.max).then_inc(s["q_elu"], 1)

        def batch(b, b_next, first):
            dve.wait_ge(s["o_mm"], T * b)
            q_elu(b, 0)
            q_elu(b, 1)
            if not first:
                head_norm(b - 1)
            q_elu(b, 2)
            q_elu(b, 3)
            dve.wait_ge(s["kv_mm"], b)
            if first:
                split(2)
                dve.wait_ge(s["rows_in"], 32)
                for t in range(T):
                    v_bias(b, t)
                split(3)
                routing_starts()
                ctx_lo(b, 0)
                dve.wait_ge(s["x_rest"], 16)
            else:
                ctx_lo(b, 0)
                copy_pos(b - 1)
                gated_mul(b - 1, 0)
                gated_lo(b - 1, 0)
                gated_mul(b - 1, 1)
                gated_lo(b - 1, 1)
                v_bias(b, 0)
                gated_mul(b - 1, 2)
                gated_lo(b - 1, 2)
                v_bias(b, 1)
                gated_mul(b - 1, 3)
                gated_lo(b - 1, 3)
                v_bias(b, 2)
                v_bias(b, 3)
                ctx_lo(b, 1)
                residual(b - 1)
                ctx_lo(b, 2)
                second_stats(b - 1)
            first_norm_a(b + 1, b_next)
            if first:
                for k in range(1, K):
                    ctx_lo(b, k)
            else:
                ctx_lo(b, 3)
                second_norm(b - 1)
            first_norm_b(b + 1, b_next)
            dve.wait_ge(s["kv_mm"], b + 1)
            dve.wait_ge(s["pool_const"], 7)
            dve.tensor_tensor(kvm[:].rearrange("p k e -> p (k e)"), kv_ps[:, :],
                              head_mask[:].rearrange("p k e -> p (k e)"), ALU.mult).then_inc(s["kv_evac"], 1)
            first_norm_lo(b + 1)
            if first:
                routing_positions()
            stats(1, lambda t: on[:, t], "o_stat", "o_aggr", T * b, "o_copy")

        def signs_of(g, j):
            dve.wait_ge(s[f"unit_in{j}"], 16 * (g + 1))
            dve.wait_ge(s["unit_mm"], 12 * g)
            dve.tensor_scalar(signs[:, j, 0], unit_slot[j], thr[:, 0, j:j + 1], None, ALU.is_gt).then_inc(s["sign_a"], 1)
            dve.tensor_scalar(signs[:, j, 1], unit_slot[j], thr[:, 1, j:j + 1], -1.0, ALU.is_lt,
                              ALU.mult).then_inc(s["sign_b"], 1)

        batch(0, 1, True)
        with dve.Fori(1, B - 1) as b:
            batch(b, b + 1, False)
        batch(B - 1, 0, False)

        dve.wait_ge(s["abs_done"], 3 * B)
        dve.tensor_reduce(abssum[:, :], absacc[:, :, :], AX.X, ALU.add).then_inc(s["scale_step"], 1)
        head_norm(B - 1)
        dve.wait_ge(s["abs_mm"], 1)
        dve.tensor_scalar(qs[:, :], prep[:, 0:3], 1.0 / (FF * D), Q_EPS, ALU.mult, ALU.add).then_inc(s["scale_step"], 1)
        dve.wait_ge(s["scale_step"], 2)
        dve.tensor_scalar(thr[:, 0], qs[:, :], 0.5, None, ALU.mult).then_inc(s["scale_step"], 1)
        dve.tensor_scalar(thr[:, 1], qs[:, :], -0.5, None, ALU.mult).then_inc(s["scale_step"], 1)
        dve.tensor_tensor(hk[:, 1:2], qs[:, 0:1], qs[:, 1:2], ALU.mult).then_inc(s["scale_step"], 1)
        dve.wait_ge(s["scale_step"], 5)
        dve.tensor_scalar(hk[:, 1:2], hk[:, 1:2], qs[:, 2:3], HID_SCALE, ALU.mult, ALU.mult).then_inc(s["scale_step"], 1)
        dve.reciprocal(hk[:, 0:1], qs[:, 0:1]).then_inc(s["scale_step"], 1)
        dve.wait_ge(s["scale_step"], 7)
        dve.tensor_scalar(hk[:, 0:1], hk[:, 0:1], 1.0 / HID_SCALE, None, ALU.mult).then_inc(s["scale_step"], 1)
        dve.wait_ge(s["scale_step"], 8)
        signs_of(0, 0)

        copy_pos(B - 1)
        for k in range(K):
            gated_mul(B - 1, k)
            gated_lo(B - 1, k)
        signs_of(0, 1)
        signs_of(0, 2)
        residual(B - 1)
        second_stats(B - 1)
        signs_of(1, 0)
        second_norm(B - 1)
        signs_of(1, 1)
        signs_of(1, 2)

        def xs_lo(i):
            dve.wait_ge(s["xs_hi"], i + 1)
            dve.tensor_tensor(xsT[:, 1], tx_ps[:, :], xsT[:, 0], ALU.subtract).then_inc(s["xs_lo"], 1)

        def y_copy(i, slot, uses):
            dve.wait_ge(s["y_mm"], i + 1)
            dve.wait_ge(s[f"ys_out{slot}"], 16 * uses)
            dve.tensor_scalar(ys_slot[slot], y_ps[:, :], CTX_SCALE ** -2, None, ALU.mult).then_inc(s["y_evac"], 1)

        def tile_step(i, quant, prev_slot, prev_uses):
            dve.wait_ge(s["z_act"], i + 1)
            dve.wait_ge(s["h_hi"], i)
            dve.tensor_tensor(h32, z_ps[:, :], sil, ALU.mult).then_inc(s["h_mul"], 1)
            if quant is not None:
                signs_of(*quant)
            if prev_slot is not None:
                y_copy(i - 1, prev_slot, prev_uses)
            xs_lo(i + 1)
            dve.wait_ge(s["h_hi"], i + 1)
            dve.tensor_tensor(hT[:, 1], th_ps[:, :], hT[:, 0], ALU.subtract).then_inc(s["h_lo"], 1)

        xs_lo(0)
        tile_step(0, None, None, None)
        for j in range(3):
            tile_step(j + 1, (2, j), j, 0)
        with dve.Fori(1, 6) as g:
            for j in range(3):
                tile_step(3 * g + j + 1, None, j, g)
        signs_of(3, 0)
        y_copy(SLOTS - 1, 0, 6)
        signs_of(3, 1)
        signs_of(3, 2)

        def x3_lo(b, t):
            dve.wait_ge(s["x3_hi"], T * b + t + 1)
            cut = bass.ds(t * P, P)
            hi = x3T[:, bass.ds(b, 1), 0, :, cut].rearrange("p a k s -> p (a k) s")
            lo = x3T[:, bass.ds(b, 1), 1, :, cut].rearrange("p a k s -> p (a k) s")
            dve.tensor_tensor(lo, t3_ps[:, :].rearrange("p (k s) -> p k s", k=K), hi, ALU.subtract).then_inc(s["x3_lo"], 1)

        dve.wait_ge(s["scattered"], 16 * NT)
        dve.tensor_copy(pos_now[:, :], pos[:, 0:T]).then_inc(s["pos3_copied"], 1)
        dve.wait_ge(s["y_in_first"], 16 * T)
        for t in range(T):
            dve.tensor_tensor(x_tile(t), n2[:, t], x_tile(t), ALU.add).then_inc(s["y_added"], 1)
        stats(0, x_tile, "x3_stat", "x3_aggr", 0, "y_added")
        dve.wait_ge(s["rs3_first"], 2)
        for t in range(T):
            normalise(0, nrm[:, t], x_tile(t), t, "x3_norm")
        for t in range(T):
            x3_lo(0, t)

        def x3_sum(b, t):
            i = T * b + t
            dve.wait_ge(s["y_in"], (i - T) * 16 + 16)
            dve.tensor_tensor(x_tile(i), n2[:, 0], x_tile(i), ALU.add).then_inc(s["y_added"], 1)
            wait_apart(dve, "y_added", i + 1)
            dve.bn_stats(st[0][:, 0], x_tile(i)).then_inc(s["x3_stat"], 1)
            wait_apart(dve, "x3_stat", i + 1)
            dve.bn_aggr(mv[0][:, 0], st[0][:, 0]).then_inc(s["x3_aggr"], 1)

        def x3_normalise(b, t):
            i = T * b + t
            dve.wait_ge(s["rs3"], 2 * (i - T) + 2)
            dve.wait_ge(s["t3_mm"], i)
            normalise(0, nrm[:, 0], x_tile(i), 0, "x3_norm")

        def next_pos(i):
            dve.tensor_copy(pos_now[:, 0:1], pos[:, bass.ds(i, 1)]).then_inc(s["pos3_copied"], 1)

        def finish(b):
            dve.wait_ge(s["down_mm"], C * b + C)
            for t in range(T):
                dve.wait_ge(s[f"out_done{t}"], 16 * b)
                dve.scalar_tensor_tensor(out=out_slot[t], in0=ffy_ps[t][:, :], scalar=hk[:, 1:2],
                                         in1=x_tile(T * b + t), op0=ALU.mult, op1=ALU.add).then_inc(s["out_made"], 1)

        def group(b, t, begins, first, nxt, more):
            for cc in range(4):
                cf = C * b + 4 * t + cc
                if begins and cc == 1 and not first:
                    finish(b - 1)
                if nxt and cc == 1:
                    x3_sum(b + 1, t)
                    if more:
                        next_pos(T * (b + 1) + t + 1)
                if nxt and cc == 2:
                    x3_normalise(b + 1, t)
                dve.wait_ge(s["up_act"], cf + 1)
                dve.wait_ge(s["gate_mm"], cf + 1)
                dve.wait_ge(s["hid_hi"], cf)
                dve.wait_ge(s["hid_lo"], cf)
                dve.scalar_tensor_tensor(out=h32, in0=sil, scalar=hk[:, 0:1], in1=gate_ps[:, :], op0=ALU.mult,
                                         op1=ALU.mult).then_inc(s["hid_mul"], 1)
                dve.wait_ge(s["hid_hi"], cf + 1)
                dve.tensor_tensor(hid[:, cc % 2, 1], h32, hid[:, cc % 2, 0], ALU.subtract).then_inc(s["hid_lo"], 1)
                if nxt and cc == 3:
                    x3_lo(b + 1, t)

        def batch3(b, first, nxt):
            group(b, 0, True, first, nxt, True)
            with dve.Fori(1, T) as t:
                group(b, t, False, False, nxt, True)

        next_pos(T)
        batch3(0, True, True)
        with dve.Fori(1, B - 1) as b:
            batch3(b, False, True)
        batch3(B - 1, False, False)
        finish(B - 1)

    @block.tensor
    def _(pe):
        def transposes(dst, src, m=None):
            for i in range(4):
                last = pe.transpose(dst[:, i * P:(i + 1) * P], src(i), ident[:, :])
            return last

        def product(dst, lhs, rhs):
            n = 0
            for k in range(K):
                for i, j in PARTS:
                    last = pe.matmul(dst, lhs(i, j, k), rhs(i, j, k), start=(n == 0), stop=(n == 3 * K - 1))
                    n += 1
            return last

        def first_norm(b1):
            for t in range(T):
                pe.wait_ge(s["x_norm"], T * b1 + t + 1)
                if t >= 2:
                    pe.wait_ge(s["x_lo"], T * b1 + t - 1)
                transposes(tr[t % 2], lambda k: nrm[:, t, k * P:(k + 1) * P]).then_inc(s["t1_mm"], 1)

        def ctx_part(b, k):
            pe.wait_ge(s["ctx_lo"], 4 * b + k)
            transposes(prep, lambda r: stage[:, 0, r, k * P:(k + 1) * P]).then_inc(s["ctx_mm"], 1)

        def head_norm(b):
            pe.wait_ge(s["o_norm"], T * b + T)
            for k in range(K):
                if k < 2:
                    pe.wait_ge(s["x_lo"], T * (b + 1) + 3 + k)
                else:
                    pe.wait_ge(s["n_aff"], K * b + k - 1)
                transposes(tr[k % 2], lambda t: on[:, t, k * P:(k + 1) * P]).then_inc(s["tn_mm"], 1)

        def project(b, bank_free):
            pe.wait_ge(s["w_lo"], 4)
            pe.wait_ge(s["a_lo"], K * b + K)
            for t in range(T):
                if t < 2:
                    if bank_free is not None:
                        pe.wait_ge(s["v_bias"], bank_free + t)
                else:
                    pe.wait_ge(s["x1_done"], T * b + t - 1)
                cut = slice(t * P, (t + 1) * P)
                product(acc[t % 2][:, :], lambda i, j, k: aT[:, i, k, cut],
                        lambda i, j, k: w_att[:, 3, j, k]).then_inc(s["wo_mm"], 1)

        def batch(b, first):
            pe.wait_ge(s["x_lo"], T * b + T)
            pe.wait_ge(s["w_lo"], 1)
            for m in range(K):
                if m < 2:
                    if not first:
                        pe.wait_ge(s["u_act"], K * (b - 1) + 3 + m)
                else:
                    pe.wait_ge(s["q_elu"], K * b + m - 1)
                product(acc[m % 2][:, :], lambda i, j, k: w_att[:, 0, j, k, m * P:(m + 1) * P],
                        lambda i, j, k: xT[:, i, k]).then_inc(s["q_mm"], 1)
            if first:
                routing_sums()
            else:
                pe.wait_ge(s["stage_in0"], 32 * b + 16)
                ctx_part(b, 0)
                head_norm(b - 1)
            pe.wait_ge(s["w_lo"], 2)
            for t in range(T):
                if t < 2:
                    pe.wait_ge(s["q_elu"], K * b + 3 + t)
                else:
                    pe.wait_ge(s["v_bias"], T * b + t - 1)
                cut = slice(t * P, (t + 1) * P)
                product(acc[t % 2][:, :], lambda i, j, k: xT[:, i, k, cut],
                        lambda i, j, k: w_att[:, 1, j, k]).then_inc(s["v_mm"], 1)
            if not first:
                ctx_part(b, 1)
                project(b - 1, T * b + 3)
                ctx_part(b, 2)
            for t in range(T):
                if t < 2:
                    if first:
                        pe.wait_ge(s["x_lo"], 3 + t)
                    else:
                        pe.wait_ge(s["n_aff"], K * (b - 1) + 3 + t)
                else:
                    pe.wait_ge(s["k_copy"], T * b + t - 1)
                transposes(tr[t % 2], lambda k: qT[:, k, t * P:(t + 1) * P]).then_inc(s["tk_mm"], 1)
            if first:
                pe.wait_ge(s["stage_in0"], 16)
                ctx_part(b, 0)
            else:
                ctx_part(b, 3)
            pe.wait_ge(s["w_lo"], 3)
            for m in range(K):
                if m < 2:
                    if first:
                        pe.wait_ge(s["v_bias"], 3 + m)
                    else:
                        pe.wait_ge(s["x1_done"], T * (b - 1) + 3 + m)
                else:
                    pe.wait_ge(s["u_act"], K * b + m - 1)
                product(acc[m % 2][:, :], lambda i, j, k: w_att[:, 2, j, k, m * P:(m + 1) * P],
                        lambda i, j, k: xT[:, i, k]).then_inc(s["u_mm"], 1)
                if first and m < 3:
                    ctx_part(b, m + 1)
            pe.wait_ge(s["k_copy"], T * b + T)
            pe.wait_ge(s["v_act"], T * b + T)
            pe.wait_ge(s["kv_evac"], b)
            if first:
                pe.wait_ge(s["route_read"], 1)
            for m in range(K):
                cut = slice(m * P, (m + 1) * P)
                for t in range(T):
                    last = pe.matmul(kv_ps[:, cut], kk[:, t, cut], vv[:, t, cut], start=(t == 0), stop=(t == T - 1))
            last.then_inc(s["kv_mm"], 1)
            first_norm(b + 1)
            pe.wait_ge(s["kv_evac"], b + 1)
            for t in range(T):
                if t < 2:
                    if not first:
                        pe.wait_ge(s["o_copy"], T * (b - 1) + 3 + t)
                else:
                    pe.wait_ge(s["o_copy"], T * b + t - 1)
                for k in range(K):
                    cut = slice(k * P, (k + 1) * P)
                    last = pe.matmul(o_ps[t % 2][:, cut], qT[:, k, t * P:(t + 1) * P], kvm[:, k], start=True, stop=True)
                last.then_inc(s["o_mm"], 1)

        def routing_sums():
            pe.wait_ge(s["route_step"], E + 3)
            pe.wait_ge(s["pool_const"], 3)
            flat = member[:, :, :].rearrange("p e c -> p (e c)")
            n = E * NT
            pe.matmul(kv_ps[:, 0:n], ones[:, :], flat, start=True, stop=True).then_inc(s["route_mm"], 1)
            pe.matmul(kv_ps[:, n:2 * n], tri[:, :], flat, start=True, stop=True).then_inc(s["route_mm"], 1)

        def unit_transposes(g, j):
            pe.wait_ge(s["sign_b"], 3 * g + j + 1)
            pe.wait_ge(s["unit_copy"], T * (3 * g + j))
            for r in range(T):
                for q in range(T):
                    cut = slice(q * P, (q + 1) * P)
                    for h in range(2):
                        last = pe.matmul(q_ps[r][:, cut], signs[:, j, h, r, cut], ident_b[:, :],
                                         start=(h == 0), stop=(h == 1))
                last.then_inc(s["unit_mm"], 1)

        pe.wait_ge(s["ident_made"], 1)
        first_norm(0)
        batch(0, True)
        with pe.Fori(1, B) as b:
            batch(b, False)
        pe.wait_ge(s["scale_step"], 1)
        pe.wait_ge(s["ctx_lo"], 4 * B)
        pe.matmul(prep[:, 0:3], ones[:, :], abssum[:, :], start=True, stop=True).then_inc(s["abs_mm"], 1)
        pe.wait_ge(s["scale_step"], 2)
        pe.wait_ge(s["o_copy"], NT)
        unit_transposes(0, 0)
        head_norm(B - 1)
        unit_transposes(0, 1)
        project(B - 1, None)
        unit_transposes(0, 2)
        for j in range(3):
            unit_transposes(1, j)

        def xs_transpose(i, slot, slot_count):
            pe.wait_ge(s[f"xs_in{slot}"], 16 * slot_count)
            pe.wait_ge(s["xs_lo"], i)
            transposes(tx_ps, lambda k: xs_slot[slot][:, k * P:(k + 1) * P]).then_inc(s["tx_mm"], 1)

        def expert(i):
            return pe.value_load(tile_expert[0:1, bass.ds(i, 1)], min_val=0, max_val=E - 1)

        def moe(dst, lhs, e):
            return product(dst, lambda i, j, k: lhs[:, i, k * P:(k + 1) * P],
                           lambda i, j, k: w_moe[:, bass.ds(e, 1), j, k].rearrange("p a d -> p (a d)"))

        def second(i):
            e = expert(i)
            pe.wait_ge(s["h_lo"], i + 1)
            pe.wait_ge(s["y_evac"], i)
            moe(y_ps[:, :], hT, e).then_inc(s["y_mm"], 1)

        def tile_step(i, quant, slot, slot_count, first):
            e = expert(i)
            pe.wait_ge(s["xs_lo"], i + 1)
            pe.wait_ge(s["h_mul"], i)
            moe(z_ps[:, :], xsT, e).then_inc(s["z_mm"], 1)
            if not first:
                second(i - 1)
            xs_transpose(i + 1, slot, slot_count)
            pe.wait_ge(s["h_mul"], i + 1)
            pe.wait_ge(s["h_lo"], i)
            transposes(th_ps, lambda k: h32[:, k * P:(k + 1) * P]).then_inc(s["th_mm"], 1)
            if quant is not None:
                unit_transposes(*quant)

        xs_transpose(0, 0, 1)
        tile_step(0, None, 1, 1, True)
        for j in range(3):
            tile_step(j + 1, (2, j), (j + 2) % 3, 1 + (j + 2) // 3, False)
        with pe.Fori(1, 6) as g:
            for j in range(3):
                tile_step(3 * g + j + 1, None, (j + 2) % 3, g + 1 + (j + 2) // 3, False)
        second(SLOTS - 1)
        for j in range(3):
            unit_transposes(3, j)

        def x3_transpose(i, t):
            pe.wait_ge(s["x3_norm"], i + 1)
            pe.wait_ge(s["x3_lo"], i)
            transposes(t3_ps, lambda k: nrm[:, t, k * P:(k + 1) * P]).then_inc(s["t3_mm"], 1)

        def two_pass(dst, w, cf_c, b):
            for k in range(K):
                for i in range(2):
                    last = pe.matmul(dst, w[:, bass.ds(cf_c, 1), k * P:(k + 1) * P].rearrange("p a n -> p (a n)"),
                                     x3T[:, bass.ds(b, 1), i, k].rearrange("p a s -> p (a s)"),
                                     start=(k == 0 and i == 0), stop=(k == K - 1 and i == 1))
            return last

        def down(cf, c, parity, start, stop):
            pe.wait_ge(s["hid_lo"], cf + 1)
            for t in range(T):
                for i in range(2):
                    last = pe.matmul(ffy_ps[t][:, :], hid[:, parity, i, t * P:(t + 1) * P],
                                     tern[2][:, bass.ds(c, 1)].rearrange("p a n -> p (a n)"),
                                     start=(start and i == 0), stop=(stop and i == 1))
            last.then_inc(s["down_mm"], 1)

        def group(b, t, begins, first, nxt):
            for cc in range(4):
                c = 4 * t + cc
                cf = C * b + c
                begin = first and cc == 0
                if not begin:
                    pe.wait_ge(s["up_act"], cf)
                two_pass(up_ps[:, :], tern[0], c, b).then_inc(s["up_mm"], 1)
                if not begin:
                    pe.wait_ge(s["hid_mul"], cf)
                two_pass(gate_ps[:, :], tern[1], c, b).then_inc(s["gate_mm"], 1)
                if begins and cc == 0:
                    if not first:
                        down(cf - 1, C - 1, 1, False, True)
                else:
                    if begins and cc == 1 and not first:
                        pe.wait_ge(s["out_made"], T * b)
                    down(cf - 1, c - 1, (cc - 1) % 2, begins and cc == 1, False)
                if nxt and cc == 2:
                    x3_transpose((b + 1) * T + t, 0)

        pe.wait_ge(s["unit_copy"], 12 * T)
        for t in range(T):
            x3_transpose(t, t)

        def batch3(b, first, nxt):
            pe.wait_ge(s["x3_lo"], T * b + T)
            group(b, 0, True, first, nxt)
            with pe.Fori(1, T) as t:
                group(b, t, False, False, nxt)

        batch3(0, True, True)
        with pe.Fori(1, B - 1) as b:
            batch3(b, False, True)
        batch3(B - 1, False, False)
        down(C * B - 1, C - 1, 1, False, True)

    es.close()


_INS = ['x', 'itok_BxS_13_99985', 'ctx_2048', 'L0_attn_Wqk', 'L0_attn_bqk', 'L0_attn_Wv', 'L0_attn_bv', 'L0_attn_Wu',
        'L0_attn_bu', 'L0_attn_Wo', 'L0_attn_bo', 'L0_attn_ln_g', 'L0_attn_ln_b', 'L0_ffn_W_up', 'L0_ffn_W_gate',
        'L0_ffn_W_down']


def kernel(**inputs):
    import concourse.bacc as _bacc
    from concourse.bass_utils import run_bass_kernel_spmd as _run

    nc = _bacc.Bacc("TRN2", target_bir_lowering=False, num_devices=1)
    arrays, args = {}, []
    for name in _INS:
        a = np.ascontiguousarray(inputs[name])
        arrays[f"in_{name}_dram"] = a
        args.append(nc.dram_tensor(f"in_{name}_dram", a.shape, mybir.dt.from_np(a.dtype), kind="ExternalInput").ap())
    args.append(nc.dram_tensor("out_0_dram", (B, S, D), F32, kind="ExternalOutput").ap())
    decoder(nc, *args)
    r = _run(nc, [arrays], core_ids=[0])
    return r.results[0]["out_0_dram"]
```

```python
from contextlib import ExitStack

import numpy as np

import concourse.bass as bass
from concourse import mybir

ALU = mybir.AluOpType
ACT = mybir.ActivationFunctionType
AX = mybir.AxisListType
F32 = mybir.dt.float32
F16 = mybir.dt.float16
BF16 = mybir.dt.bfloat16
I32 = mybir.dt.int32

P = 128
B, S, D = 4, 512, 512
FF = 2048
K = D // P
T = S // P
NT = B * T
HD = 32
E = 4
VOCAB = 25000
SLOTS = NT + E - 1
C = FF // P
CTX_SCALE = 256.0
HID_SCALE = 8.0
LN_EPS = 1e-5
Q_EPS = 1e-8
PARTS = ((0, 0), (1, 0), (0, 1))


def decoder(nc, x, itok, ctx_w, Wqk, bqk, Wv, bv, Wu, bu, Wo, bo, ln_g, ln_b, W_up, W_gate, W_down, out):
    es = ExitStack()

    def sb(name, shape, dt=F32):
        return es.enter_context(nc.sbuf_tensor(name, shape, dt))

    def sem(name):
        return es.enter_context(nc.semaphore(name))

    x_v = x.rearrange("b (t p) d -> p (b t) d", p=P)
    out_v = out.rearrange("b (t p) d -> p (b t) d", p=P)
    tok_v = itok.rearrange("b (t p) -> p (b t)", p=P)
    ctx_v = ctx_w.rearrange("e (r p) d -> p e r d", p=P)
    att_v = [w.rearrange("(k p) n -> p k n", p=P) for w in (Wqk, Wv, Wu, Wo)]
    unit_v = [W_up.rearrange("(g r p) d -> p g r d", r=T, p=P),
              W_gate.rearrange("(g r p) d -> p g r d", r=T, p=P),
              W_down.rearrange("(g p) (r d) -> p g r d", p=P, r=T)]
    column = lambda v: v.rearrange("(k p) -> p k", p=P)
    xs_dram = nc.dram_tensor("sorted_tokens", ((SLOTS + 1) * P, D), F32, kind="Internal").ap()
    ys_dram = nc.dram_tensor("sorted_outputs", (SLOTS * P, D), F32, kind="Internal").ap()
    xs_v = xs_dram.rearrange("(c p) d -> p c d", p=P)
    ys_v = ys_dram.rearrange("(c p) d -> p c d", p=P)

    resid = sb("resid", [P, NT, D])
    w_att = sb("w_att", [P, 4, 2, K, D], F16)
    w_moe = sb("w_moe", [P, E, 2, K, D], F16)
    region = sb("region", [P, 6, T, D])
    stage = sb("stage", [P, 2, T, D])
    nrm = sb("nrm", [P, T, D])
    n2 = sb("n2", [P, T, D])
    tmp = sb("tmp", [P, 2, D])
    tmpA = sb("tmpA", [P, 2, D])
    a32 = sb("a32", [P, 2, D])
    kvm = sb("kvm", [P, K, P])
    xT = sb("xT", [P, 2, K, S], F16)
    bv_bc = sb("bv_bc", [P, D])
    bo_bc = sb("bo_bc", [P, D])
    head_mask = sb("head_mask", [P, K, P])
    cols = sb("cols", [P, 4, K])
    ident = sb("ident", [P, P])
    ident_b = sb("ident_b", [P, P], BF16)
    ones = sb("ones", [P, P])
    tri = sb("tri", [P, P])
    halfs = sb("halfs", [P, T])
    st = [sb(f"st{i}", [P, T, 6]) for i in range(3)]
    mv = [sb(f"mv{i}", [P, T, 2]) for i in range(3)]
    ve = [sb(f"ve{i}", [P, T]) for i in range(3)]
    rs = [sb(f"rs{i}", [P, T]) for i in range(3)]
    absacc = sb("absacc", [P, 3, B])
    abssum = sb("abssum", [P, 3])
    qs = sb("qs", [P, 3])
    thr = sb("thr", [P, 2, 3])
    hk = sb("hk", [P, 2])
    tok = sb("tok", [P, NT], I32)
    tokf = sb("tokf", [P, NT])
    pad_i = sb("pad_i", [P, 2, E], I32)
    pad_f = sb("pad_f", [P, E])
    base = sb("base", [P, E])
    pos_f = sb("pos_f", [P, NT])
    pos = sb("pos", [P, NT + 1], I32)
    pos_now = sb("pos_now", [P, T], I32)
    starts_i = sb("starts_i", [1, SLOTS], I32)
    starts = sb("starts", [1, SLOTS])
    te_f = sb("te_f", [1, E, SLOTS])
    tile_expert = sb("tile_expert", [1, SLOTS], I32)

    rt = region[:, 5, 0, 0:(3 * E + 1 + E) * NT].rearrange("p (e c) -> p e c", c=NT)
    ge, member, before = rt[:, 0:E + 1], rt[:, E + 1:2 * E + 1], rt[:, 2 * E + 1:3 * E + 1]
    scan = region[:, 5, 1, 0:2 * E * NT].rearrange("p (i e c) -> p i e c", i=2, e=E)
    qT, kk, vv, uT, on = [region[:, i] for i in range(5)]
    aT = region[:, 5].rearrange("p a b -> p (a b)").bitcast(F16).rearrange("p (h k s) -> p h k s", h=2, k=K)
    tern = [region[:, 2 * i:2 * i + 2].rearrange("p a b c -> p (a b c)").bitcast(BF16)
            .rearrange("p (c n) -> p c n", c=C) for i in range(3)]
    signs = w_att[:].rearrange("p a b c d -> p (a b c d)")[:, 0:6 * FF].bitcast(BF16).rearrange(
        "p (j s r d) -> p j s r d", j=3, s=2, r=T)
    x3T = w_att
    att_slot = [stage[:, 0], stage[:, 1], on, n2[:, :, :]]
    out_slot = [stage[:, 0, t] for t in range(T)]
    unit_slot = [stage[:, 0], stage[:, 1], nrm[:, :, :]]
    xs_slot = [n2[:, i] for i in range(3)]
    ys_slot = [n2[:, 3], a32[:, 0], a32[:, 1]]
    sil, h32 = tmp[:, 0], tmp[:, 1]
    tA = tmpA[:].rearrange("p a b -> p (a b)").bitcast(F16).rearrange("p (i h n) -> p i h n", i=2, h=2)
    xsT, hT = tA[:, 0], tA[:, 1]
    hid = tA

    ps = [es.enter_context(nc.psum_tensor(f"bank{i}", [P, 512], F32)) for i in range(8)]
    acc, tr, kv_ps, o_ps, prep = ps[0:2], ps[2:4], ps[4], ps[5:7], ps[7]
    z_ps, y_ps, tx_ps, th_ps, q_ps = ps[0], ps[1], ps[2], ps[3], ps[4:8]
    ffy_ps, up_ps, gate_ps, t3_ps = ps[0:4], ps[4], ps[5], ps[6]

    names = """x_first0 x_first1 x_first2 x_first3 x_rest cols_in rows_in tok_in att_in0 att_in1 att_in2 att_in3 stage_in0 stage_in1
        zeroed scattered xs_in0 xs_in1 xs_in2 unit_in0 unit_in1 unit_in2 ys_out0 ys_out1 ys_out2 ys_out_last y_in y_in_first0 y_in_first1 y_in_first2 y_in_first3
        out_done0 out_done1 out_done2 out_done3
        ident_made pool_const zero_src starts_made bias_added rs1_first rs1 rs_o rs2 rs2_last rs3 rs3_first
        w_hi w_lo ctx_mm ctx_hi ctx_lo abs_done abs_mm scale_step
        route_step route_mm route_read route_ready
        x_stat x_aggr x_norm t1_mm x_hi x_lo
        q_mm q_exp q_clip q_elu tn_mm n_aff a_mul a_hi a_lo v_mm v_bias v_act wo_mm x1_done
        x2_stat x2_aggr x2_norm pos_copied tk_mm k_copy u_mm u_act kv_mm kv_evac o_mm o_copy o_stat o_aggr o_norm
        tx_mm xs_hi xs_lo z_mm z_act h_mul th_mm h_hi h_lo y_mm y_evac sign_a sign_b unit_mm unit_copy
        y_added x3_stat x3_aggr x3_norm t3_mm x3_hi x3_lo pos3_copied
        up_mm gate_mm up_act hid_mul hid_hi hid_lo down_mm out_made""".split()
    s = {n: sem(n) for n in names}

    def wait_apart(eng, name, value):
        if not isinstance(value, int):
            eng.lower_val(value)
        eng.wait_ge(s["zero_src"], 1)
        eng.wait_ge(s[name], value)

    block = es.enter_context(nc.Block())

    @block.sync
    def _(sp):
        for t in range(T):
            sp.dma_start(resid[:, t], x_v[:, t]).then_inc(s[f"x_first{t}"], 16)
        sp.dma_start(att_slot[0], att_v[0]).then_inc(s["att_in0"], 16)
        for i, v in enumerate((bqk, bu, ln_g, ln_b)):
            sp.dma_start(cols[:, i], column(v), allow_slow_non_contiguous=True).then_inc(s["cols_in"], 16)
        sp.dma_start(tok[:, :], tok_v, allow_slow_non_contiguous=True).then_inc(s["tok_in"], 16)
        for m in (1, 2, 3):
            sp.dma_start(att_slot[m], att_v[m]).then_inc(s[f"att_in{m}"], 16)
        sp.dma_start(bv_bc[:, :], bv.partition_broadcast(P)).then_inc(s["rows_in"], 16)
        sp.dma_start(bo_bc[:, :], bo.partition_broadcast(P)).then_inc(s["rows_in"], 16)
        sp.dma_start(resid[:, T:NT], x_v[:, T:NT]).then_inc(s["x_rest"], 16)

        def expert_weights(b):
            sp.dma_start(stage[:, 0], ctx_v[:, bass.ds(b, 1)].rearrange("p a r d -> p (a r) d")).then_inc(
                s["stage_in0"], 16)

        def summed_unit(b, j, slot):
            sp.dma_start(stage[:, slot], unit_v[j][:, bass.ds(b, 1)].rearrange("p a r d -> p (a r) d")).then_inc(
                s[f"stage_in{slot}"], 16)

        def weights(b, first):
            if first:
                sp.wait_ge(s["w_lo"], 1)
                expert_weights(b)
                sp.wait_ge(s["w_lo"], 2)
                summed_unit(b, 0, 1)
                sp.wait_ge(s["zero_src"], 1)
                with sp.Fori(0, (SLOTS + 1) // 2) as i:
                    sp.dma_start(xs_v[:, bass.ds(2 * i, 2)], a32[:, :, :]).then_inc(s["zeroed"], 16)
            else:
                sp.wait_ge(s["abs_done"], 3 * b - 1)
                expert_weights(b)
                sp.wait_ge(s["abs_done"], 3 * b)
                summed_unit(b, 0, 1)
            sp.wait_ge(s["ctx_mm"], 4 * b + 4)
            summed_unit(b, 1, 0)
            sp.wait_ge(s["abs_done"], 3 * b + 1)
            summed_unit(b, 2, 1)

        weights(0, True)
        with sp.Fori(1, B) as b:
            weights(b, False)

        def unit(g, j):
            sp.dma_start(unit_slot[j], unit_v[j][:, bass.ds(g, 1)].rearrange("p a r d -> p (a r) d")).then_inc(
                s[f"unit_in{j}"], 16)

        def sorted_tile(i, slot):
            sp.dma_start(xs_slot[slot], xs_v[:, bass.ds(i, 1)].rearrange("p a d -> p (a d)")).then_inc(
                s[f"xs_in{slot}"], 16)

        sp.wait_ge(s["abs_done"], 3 * B - 1)
        unit(0, 0)
        sp.wait_ge(s["abs_done"], 3 * B)
        unit(0, 1)
        sp.wait_ge(s["t1_mm"], T * B)
        unit(0, 2)
        for j in range(3):
            sp.wait_ge(s["sign_b"], j + 1)
            unit(1, j)
        sp.wait_ge(s["scattered"], 16 * NT)
        for i in range(3):
            sorted_tile(i, i)
        with sp.Fori(2, 4) as g:
            for j in range(3):
                sp.wait_ge(s["sign_b"], 3 * (g - 1) + j + 1)
                unit(g, j)
                sp.wait_ge(s["tx_mm"], 3 * (g - 2) + j + 1)
                sorted_tile(3 * (g - 1) + j, j)
        with sp.Fori(2, 5) as g:
            for j in range(3):
                sp.wait_ge(s["tx_mm"], 3 * g + j + 1)
                sorted_tile(3 * g + j + 3, j)
        for i in (18, 19):
            sp.wait_ge(s["tx_mm"], i - 2)
            sorted_tile(i, i % 3)

        sp.wait_ge(s["y_evac"], SLOTS)
        sp.dma_start(ys_v[:, SLOTS - 1], ys_slot[0]).then_inc(s["ys_out_last"], 16)

        with sp.Fori(0, B) as b:
            for t in range(T):
                sp.wait_ge(s["out_made"], T * b + t + 1)
                sp.dma_start(out_v[:, bass.ds(T * b + t, 1)].rearrange("p a d -> p (a d)"), out_slot[t]).then_inc(
                    s[f"out_done{t}"], 16)
        for t in range(T):
            sp.wait_ge(s[f"out_done{t}"], 16 * B)

    @block.gpsimd
    def _(pool):
        pool.memset(ones[:, :], 1.0).then_inc(s["pool_const"], 1)
        pool.memset(halfs[:, :], -0.5).then_inc(s["pool_const"], 1)
        pool.wait_ge(s["pool_const"], 2)
        pool.affine_select(out=ident[:, :], in_=ones[:, :], compare_op=ALU.is_equal, fill=0.0, base=0,
                           pattern=[[-1, P]], channel_multiplier=1).then_inc(s["ident_made"], 1)
        pool.affine_select(out=tri[:, :], in_=ones[:, :], compare_op=ALU.is_gt, fill=0.0, base=0,
                           pattern=[[1, P]], channel_multiplier=-1).then_inc(s["pool_const"], 1)
        pool.memset(a32[:, :, :], 0.0).then_inc(s["zero_src"], 1)

        def late_constants():
            pool.memset(head_mask[:, :, :], 1.0).then_inc(s["pool_const"], 1)
            pool.wait_ge(s["pool_const"], 4)
            hm = head_mask[:].rearrange("p k (j e) -> p k j e", e=HD)
            pool.affine_select(out=hm, in_=hm, compare_op=ALU.is_ge, fill=0.0, base=0,
                               pattern=[[0, K], [-HD, P // HD], [0, HD]], channel_multiplier=1).then_inc(s["pool_const"], 1)
            pool.wait_ge(s["pool_const"], 5)
            pool.affine_select(out=hm, in_=hm, compare_op=ALU.is_ge, fill=0.0, base=HD - 1,
                               pattern=[[0, K], [HD, P // HD], [0, HD]], channel_multiplier=-1).then_inc(s["pool_const"], 1)
            pool.tensor_copy(ident_b[:, :], ident[:, :]).then_inc(s["pool_const"], 1)
            pool.iota(starts_i[:, :], pattern=[[P, SLOTS]], base=0, channel_multiplier=0).then_inc(s["starts_made"], 1)

        def rsqrt(i, aggr, wait, tiles, done, k):
            wait_apart(pool, aggr, wait)
            pool.tensor_scalar(ve[i][:, tiles], mv[i][:, tiles, 1], LN_EPS, 0.0, ALU.add, ALU.add).then_inc(s[done], 1)
            pool.wait_ge(s[done], 2 * k + 1)
            pool.tensor_tensor(rs[i][:, tiles], ve[i][:, tiles], halfs[:, tiles], ALU.pow).then_inc(s[done], 1)

        def rsqrt_tile(i, aggr, n0, t, done):
            rsqrt(i, aggr, n0 + t + 1, slice(t, t + 1), done, t)

        def scatter(b, t):
            wait_apart(pool, "x2_norm", T * b + t + 1)
            pool.indirect_dma_start(xs_dram, bass.IndirectOffsetOnAxis(ap=pos_now[:, t:t + 1], axis=0),
                                    n2[:, t], None).then_inc(s["scattered"], 16)

        def batch(b, first, last):
            pool.wait_ge(s["x_norm"], T * b + T)
            for t in range(T):
                xt = resid[:, bass.ds(T * b + t, 1)].rearrange("p a d -> p (a d)")
                pool.tensor_tensor(xt, xt, bo_bc[:, :], ALU.add).then_inc(s["bias_added"], 1)
            if not first:
                rsqrt(2, "x2_aggr", T * b, slice(0, T), "rs2", b - 1)
                for t in range(T):
                    scatter(b - 1, t)
            if not last:
                rsqrt(0, "x_aggr", T * b + 2 * T, slice(0, T), "rs1", b)
            rsqrt(1, "o_aggr", T * b + T, slice(0, T), "rs_o", b)

        for t in range(T):
            rsqrt_tile(0, "x_aggr", 0, t, "rs1_first")
        late_constants()
        pool.wait_ge(s["rows_in"], 32)
        batch(0, True, False)
        pool.wait_ge(s["zeroed"], 16 * ((SLOTS + 1) // 2))
        with pool.Fori(1, B - 1) as b:
            batch(b, False, False)
        batch(B - 1, False, True)
        rsqrt_tile(2, "x2_aggr", T * (B - 1), 0, "rs2_last")
        for t in range(1, T):
            rsqrt_tile(2, "x2_aggr", T * (B - 1), t, "rs2_last")
            scatter(B - 1, t - 1)
        scatter(B - 1, T - 1)

        def store(i, slot, j):
            pool.wait_ge(s["y_evac"], j)
            pool.dma_start(ys_v[:, bass.ds(i, 1)].rearrange("p a d -> p (a d)"), ys_slot[slot]).then_inc(
                s[f"ys_out{slot}"], 16)

        with pool.Fori(0, 6) as g:
            for j in range(3):
                store(3 * g + j, j, 3 * g + j + 1)

        for slot in range(3):
            pool.wait_ge(s[f"ys_out{slot}"], 16 * 6)
        pool.wait_ge(s["ys_out_last"], 16)

        for t in range(T):
            pool.wait_ge(s["pos3_copied"], 1)
            pool.indirect_dma_start(n2[:, t], None, ys_dram,
                                    bass.IndirectOffsetOnAxis(ap=pos_now[:, t:t + 1], axis=0)).then_inc(
                                        s[f"y_in_first{t}"], 16)
        for t in range(T):
            rsqrt_tile(0, "x3_aggr", 0, t, "rs3_first")
        with pool.Fori(T, NT) as i:
            wait_apart(pool, "pos3_copied", i - T + 2)
            pool.indirect_dma_start(n2[:, 0], None, ys_dram,
                                    bass.IndirectOffsetOnAxis(ap=pos_now[:, 0:1], axis=0)).then_inc(s["y_in"], 16)
            rsqrt(0, "x3_aggr", i + 1, slice(0, 1), "rs3", i - T)

    @block.scalar
    def _(act):
        def first_norm(b1):
            for t in range(T):
                act.wait_ge(s["t1_mm"], T * b1 + t + 1)
                act.activation(xT[:, 0, :, t * P:(t + 1) * P], tr[t % 2].rearrange("p (k s) -> p k s", k=K),
                               ACT.Copy).then_inc(s["x_hi"], 1)

        def split(m):
            act.wait_ge(s[f"att_in{m}"], 16)
            act.activation(w_att[:, m, 0], att_slot[m], ACT.Copy).then_inc(s["w_hi"], 1)

        def ctx_hi(b, k):
            act.wait_ge(s["ctx_mm"], 4 * b + k + 1)
            act.activation(w_moe[:, bass.ds(b, 1), 0, k].rearrange("p a d -> p (a d)"), prep[:, :], ACT.Copy,
                           scale=CTX_SCALE).then_inc(s["ctx_hi"], 1)

        def affine(b, k):
            act.wait_ge(s["tn_mm"], K * b + k + 1)
            act.wait_ge(s["a_mul"], K * b + (k - 1 if k >= 2 else 0))
            act.activation(tmpA[:, k % 2], tr[k % 2][:, :], ACT.Identity, bias=cols[:, 3, k:k + 1],
                           scale=cols[:, 2, k:k + 1]).then_inc(s["n_aff"], 1)

        def gated_hi(b, k):
            act.wait_ge(s["a_mul"], K * b + k + 1)
            act.wait_ge(s["wo_mm"], T * b)
            act.activation(aT[:, 0, k], a32[:, k % 2], ACT.Copy).then_inc(s["a_hi"], 1)

        def v_act(b, t):
            act.wait_ge(s["v_bias"], T * b + t + 1)
            act.activation(vv[:, t], vv[:, t], ACT.Silu).then_inc(s["v_act"], 1)

        def magnitudes(b, j):
            slot, n = ((1, 1), (0, 2), (1, 2))[j]
            act.wait_ge(s[f"stage_in{slot}"], 32 * b + 16 * n)
            act.activation(stage[:, slot], stage[:, slot], ACT.Abs,
                           accum_out=absacc[:, j, bass.ds(b, 1)]).then_inc(s["abs_done"], 1)

        def batch(b, first, last):
            for m in range(K):
                act.wait_ge(s["q_mm"], K * b + m + 1)
                if not first or m >= 2:
                    act.wait_ge(s["q_elu"], K * b + m - 1)
                act.activation(tmp[:, m % 2], acc[m % 2][:, :], ACT.Exp, bias=cols[:, 0, m:m + 1]).then_inc(s["q_exp"], 1)
            if first:
                split(2)
                for t in range(T):
                    v_act(b, t)
                split(3)
            else:
                ctx_hi(b, 0)
                affine(b - 1, 0)
                affine(b - 1, 1)
                gated_hi(b - 1, 0)
                affine(b - 1, 2)
                gated_hi(b - 1, 1)
                v_act(b, 0)
                affine(b - 1, 3)
                gated_hi(b - 1, 2)
                v_act(b, 1)
                gated_hi(b - 1, 3)
                v_act(b, 2)
                v_act(b, 3)
                ctx_hi(b, 1)
                ctx_hi(b, 2)
            act.wait_ge(s["kv_mm"], b)
            for t in range(T):
                act.wait_ge(s["tk_mm"], T * b + t + 1)
                act.activation(kk[:, t], tr[t % 2][:, :], ACT.Copy).then_inc(s["k_copy"], 1)
            ctx_hi(b, 0 if first else 3)
            magnitudes(b, 0)
            act.wait_ge(s["a_mul"], K * b)
            for m in range(K):
                act.wait_ge(s["u_mm"], K * b + m + 1)
                act.activation(uT[:, m], acc[m % 2][:, :], ACT.Silu, bias=cols[:, 1, m:m + 1]).then_inc(s["u_act"], 1)
                if first and m < 3:
                    ctx_hi(b, m + 1)
                if m == 2:
                    magnitudes(b, 1)
            if not last:
                first_norm(b + 1)
            act.wait_ge(s["tn_mm"], K * b)
            for t in range(T):
                act.wait_ge(s["o_mm"], T * b + t + 1)
                act.activation(on[:, t], o_ps[t % 2][:, :], ACT.Copy).then_inc(s["o_copy"], 1)
            magnitudes(b, 2)

        def unit_copies(g, j):
            for r in range(T):
                act.wait_ge(s["unit_mm"], T * (3 * g + j) + r + 1)
                if j < 2:
                    dst, src = tern[j][:, bass.ds(T * g + r, 1)].rearrange("p a n -> p (a n)"), q_ps[r][:, :]
                else:
                    dst, src = tern[j][:, T * r:T * r + T, bass.ds(P * g, P)], q_ps[r].rearrange("p (c d) -> p c d", c=T)
                act.activation(dst, src, ACT.Copy).then_inc(s["unit_copy"], 1)

        split(0)
        first_norm(0)
        split(1)
        act.wait_ge(s["cols_in"], 64)
        batch(0, True, False)
        with act.Fori(1, B - 1) as b:
            batch(b, False, False)
        batch(B - 1, False, True)
        affine(B - 1, 0)
        for k in range(1, K):
            affine(B - 1, k)
            gated_hi(B - 1, k - 1)
        gated_hi(B - 1, K - 1)
        for g, j in ((0, 0), (0, 1), (0, 2), (1, 0), (1, 1)):
            unit_copies(g, j)

        def xs_hi(i):
            act.wait_ge(s["tx_mm"], i + 1)
            act.wait_ge(s["z_mm"], i)
            act.activation(xsT[:, 0], tx_ps[:, :], ACT.Copy).then_inc(s["xs_hi"], 1)

        def tile_step(i, quant):
            act.wait_ge(s["z_mm"], i + 1)
            act.wait_ge(s["h_mul"], i)
            act.activation(sil, z_ps[:, :], ACT.Silu, scale=1.0 / CTX_SCALE).then_inc(s["z_act"], 1)
            xs_hi(i + 1)
            if quant is not None:
                unit_copies(*quant)
            act.wait_ge(s["th_mm"], i + 1)
            act.wait_ge(s["y_mm"], i)
            act.activation(hT[:, 0], th_ps[:, :], ACT.Copy).then_inc(s["h_hi"], 1)

        xs_hi(0)
        tile_step(0, (1, 2))
        with act.Fori(0, 2) as g:
            for j in range(3):
                tile_step(3 * g + j + 1, (g + 2, j))
        with act.Fori(7, SLOTS) as i:
            tile_step(i, None)

        def x3_hi(b, t, bank=t3_ps):
            act.wait_ge(s["t3_mm"], T * b + t + 1)
            act.activation(x3T[:, bass.ds(b, 1), 0, :, bass.ds(t * P, P)].rearrange("p a k s -> p (a k) s"),
                           bank[:, :].rearrange("p (k s) -> p k s", k=K), ACT.Copy).then_inc(s["x3_hi"], 1)

        def group(b, t, first, nxt):
            for cc in range(4):
                cf = C * b + 4 * t + cc
                act.wait_ge(s["up_mm"], cf + 1)
                act.wait_ge(s["hid_mul"], cf)
                act.activation(sil, up_ps[:, :], ACT.Silu, scale=qs[:, 0:1]).then_inc(s["up_act"], 1)
                act.wait_ge(s["hid_mul"], cf + 1)
                if not (first and cc < 2):
                    act.wait_ge(s["down_mm"], cf - 1)
                act.activation(hid[:, cc % 2, 0], h32, ACT.Copy).then_inc(s["hid_hi"], 1)
                if nxt and cc == 3:
                    x3_hi(b + 1, t)

        for t in range(T):
            x3_hi(0, t, ps[t])

        def batch3(b, first, nxt):
            group(b, 0, first, nxt)
            with act.Fori(1, T) as t:
                group(b, t, False, nxt)

        batch3(0, True, True)
        with act.Fori(1, B - 1) as b:
            batch3(b, False, True)
        batch3(B - 1, False, False)

    @block.vector
    def _(dve):
        def tile_stats(i, t, src, stat):
            dve.bn_stats(st[i][:, t], src).then_inc(s[stat], 1)

        def aggregate(i, t, stat, n, aggr):
            wait_apart(dve, stat, n)
            dve.bn_aggr(mv[i][:, t], st[i][:, t]).then_inc(s[aggr], 1)

        def normalise(i, dst, src, t, done):
            dve.tensor_scalar(dst, src, mv[i][:, t, 0:1], rs[i][:, t:t + 1], ALU.subtract, ALU.mult).then_inc(s[done], 1)

        def x_tile(n):
            return resid[:, bass.ds(n, 1)].rearrange("p a d -> p (a d)")

        def first_stats(b1):
            for t in range(T):
                tile_stats(0, t, x_tile(T * b1 + t), "x_stat")
            for t in range(T):
                aggregate(0, t, "x_stat", T * b1 + T, "x_aggr")

        def first_norm(b1):
            dve.wait_ge(s["rs1"], 2 * b1)
            dve.wait_ge(s["t1_mm"], T * b1)
            for t in range(T):
                normalise(0, nrm[:, t], x_tile(T * b1 + t), t, "x_norm")

        def first_norm_lo(b1):
            for t in range(T):
                dve.wait_ge(s["x_hi"], T * b1 + t + 1)
                cut = slice(t * P, (t + 1) * P)
                dve.tensor_tensor(xT[:, 1, :, cut], tr[t % 2].rearrange("p (k s) -> p k s", k=K),
                                  xT[:, 0, :, cut], ALU.subtract).then_inc(s["x_lo"], 1)

        def split(m):
            dve.wait_ge(s["w_hi"], m + 1)
            dve.tensor_tensor(w_att[:, m, 1], att_slot[m], w_att[:, m, 0], ALU.subtract).then_inc(s["w_lo"], 1)

        step = [0]

        def route(ins):
            step[0] += 1
            ins.then_inc(s["route_step"], 1)
            dve.wait_ge(s["route_step"], step[0])

        def routing_members():
            dve.wait_ge(s["tok_in"], 16)
            route(dve.tensor_copy(tokf[:, :], tok[:, :]))
            dve.memset(ge[:, 0], 1.0).then_inc(s["route_step"], 1)
            dve.memset(ge[:, E], 0.0).then_inc(s["route_step"], 1)
            for e in range(1, E):
                dve.tensor_scalar(ge[:, e], tokf[:, :], float(e * (VOCAB // E)), None, ALU.is_ge).then_inc(s["route_step"], 1)
            step[0] += E + 1
            dve.wait_ge(s["route_step"], step[0])
            route(dve.tensor_tensor(member[:, :, :], ge[:, 0:E], ge[:, 1:E + 1], ALU.subtract))

        def routing_starts():
            dve.wait_ge(s["route_mm"], 2)
            route(dve.tensor_copy(scan[:, 0], kv_ps[:, 0:E * NT].rearrange("p (e c) -> p e c", e=E)))
            dve.tensor_tensor(before[:, :, :], kv_ps[:, E * NT:2 * E * NT].rearrange("p (e c) -> p e c", e=E),
                              scan[:, 0], ALU.subtract).then_inc(s["route_read"], 1)
            dve.wait_ge(s["route_read"], 1)
            a, d = 0, 1
            while d < NT:
                dve.tensor_copy(scan[:, 1 - a, :, 0:d], scan[:, a, :, 0:d]).then_inc(s["route_step"], 1)
                step[0] += 1
                route(dve.tensor_tensor(scan[:, 1 - a, :, d:NT], scan[:, a, :, d:NT], scan[:, a, :, 0:NT - d], ALU.add))
                a, d = 1 - a, 2 * d
            count = scan[:, a, :, NT - 1]
            route(dve.tensor_scalar(pad_f[:, :], count, float(P - 1), None, ALU.add))
            route(dve.tensor_copy(pad_i[:, 0], pad_f[:, :]))
            route(dve.tensor_scalar(pad_i[:, 1], pad_i[:, 0], 7, 7, ALU.logical_shift_right, ALU.logical_shift_left))
            route(dve.tensor_copy(pad_f[:, :], pad_i[:, 1]))
            route(dve.memset(base[:, :], 0.0))
            for e in range(1, E):
                route(dve.tensor_tensor(base[:, e:e + 1], base[:, e - 1:e], pad_f[:, e - 1:e], ALU.add))
            assert d == NT and a == 0

        def routing_positions():
            a = 0
            route(dve.tensor_tensor(before[:, :, :], before[:, :, :], scan[:, a], ALU.add))
            for e in range(E):
                dve.tensor_scalar(ge[:, e], before[:, e], base[:, e:e + 1], None, ALU.add).then_inc(s["route_step"], 1)
            step[0] += E
            dve.wait_ge(s["route_step"], step[0])
            route(dve.tensor_tensor(before[:, :, :], ge[:, 0:E], member[:, :, :], ALU.mult))
            route(dve.tensor_reduce(pos_f[:, :], before[:, :, :].rearrange("p e c -> p c e"), AX.X, ALU.add))
            route(dve.memset(pos[:, NT:NT + 1], 0))
            route(dve.tensor_copy(pos[:, 0:NT], pos_f[:, :]))
            dve.wait_ge(s["starts_made"], 1)
            route(dve.tensor_copy(starts[:, :], starts_i[:, :]))
            for e in range(1, E):
                dve.tensor_scalar(te_f[:, e], starts[:, :], base[0:1, e:e + 1], None, ALU.is_ge).then_inc(s["route_step"], 1)
            step[0] += E - 1
            dve.wait_ge(s["route_step"], step[0])
            route(dve.tensor_tensor(te_f[:, 0], te_f[:, 1], te_f[:, 2], ALU.add))
            route(dve.tensor_tensor(te_f[:, 1], te_f[:, 0], te_f[:, 3], ALU.add))
            dve.tensor_copy(tile_expert[:, :], te_f[:, 1]).then_inc(s["route_ready"], 1)

        def first_tile(t):
            wait_apart(dve, f"x_first{t}", 16)
            tile_stats(0, t, x_tile(t), "x_stat")
            aggregate(0, t, "x_stat", t + 1, "x_aggr")

        def first_tile_norm(t):
            dve.wait_ge(s["rs1_first"], 2 * t + 2)
            normalise(0, nrm[:, t], x_tile(t), t, "x_norm")

        first_tile(0)
        for t in range(1, T):
            first_tile(t)
            first_tile_norm(t - 1)
        first_tile_norm(T - 1)
        split(0)
        first_norm_lo(0)
        split(1)
        routing_members()
        dve.wait_ge(s["cols_in"], 64)

        def gated_mul(b, k):
            if k == 0:
                dve.wait_ge(s["zeroed"], 16 * ((SLOTS + 1) // 2))
                dve.wait_ge(s["u_act"], K * b + K)
            if k >= 2:
                dve.wait_ge(s["a_lo"], K * b + k - 1)
            dve.wait_ge(s["n_aff"], K * b + k + 1)
            dve.tensor_tensor(a32[:, k % 2], tmpA[:, k % 2], uT[:, k], ALU.mult).then_inc(s["a_mul"], 1)

        def gated_lo(b, k):
            dve.wait_ge(s["a_hi"], K * b + k + 1)
            dve.tensor_tensor(aT[:, 1, k], a32[:, k % 2], aT[:, 0, k], ALU.subtract).then_inc(s["a_lo"], 1)

        def v_bias(b, t):
            dve.wait_ge(s["v_mm"], T * b + t + 1)
            dve.tensor_tensor(vv[:, t], acc[t % 2][:, :], bv_bc[:, :], ALU.add).then_inc(s["v_bias"], 1)

        def head_norm(b):
            dve.wait_ge(s["rs_o"], 2 * b + 2)
            for t in range(T):
                normalise(1, on[:, t], on[:, t], t, "o_norm")

        def residual(b, t):
            dve.wait_ge(s["wo_mm"], T * b + t + 1)
            dve.wait_ge(s["bias_added"], T * b + t + 1)
            dve.tensor_tensor(x_tile(T * b + t), acc[t % 2][:, :], x_tile(T * b + t), ALU.add).then_inc(s["x1_done"], 1)

        def second_stats(b, t):
            wait_apart(dve, "x1_done", T * b + t + 1)
            tile_stats(2, t, x_tile(T * b + t), "x2_stat")

        def second_norm(b, t):
            dve.wait_ge(s["scattered"], 16 * T * b)
            normalise(2, n2[:, t], x_tile(T * b + t), t, "x2_norm")

        def copy_pos(b):
            dve.wait_ge(s["scattered"], 16 * T * b)
            dve.tensor_copy(pos_now[:, :], pos[:, bass.ds(T * b, T)]).then_inc(s["pos_copied"], 1)

        def ctx_lo(b, k):
            dve.wait_ge(s["ctx_hi"], 4 * b + k + 1)
            hi = w_moe[:, bass.ds(b, 1), 0, k].rearrange("p a d -> p (a d)")
            lo = w_moe[:, bass.ds(b, 1), 1, k].rearrange("p a d -> p (a d)")
            dve.scalar_tensor_tensor(out=lo, in0=prep[:, :], scalar=CTX_SCALE, in1=hi, op0=ALU.mult,
                                     op1=ALU.subtract).then_inc(s["ctx_lo"], 1)

        def q_elu(b, m):
            dve.wait_ge(s["q_exp"], K * b + m + 1)
            dve.tensor_scalar(tmp[:, m % 2], tmp[:, m % 2], 1.0, -1.0, ALU.min, ALU.add).then_inc(s["q_clip"], 1)
            dve.wait_ge(s["q_clip"], K * b + m + 1)
            dve.scalar_tensor_tensor(out=qT[:, m], in0=acc[m % 2][:, :], scalar=cols[:, 0, m:m + 1],
                                     in1=tmp[:, m % 2], op0=ALU.add, op1=ALU.max).then_inc(s["q_elu"], 1)

        def batch(b, first, last):
            dve.wait_ge(s["o_mm"], T * b)
            q_elu(b, 0)
            q_elu(b, 1)
            if not first:
                head_norm(b - 1)
            q_elu(b, 2)
            q_elu(b, 3)
            dve.wait_ge(s["kv_mm"], b)
            if first:
                split(2)
                dve.wait_ge(s["rows_in"], 32)
                for t in range(T):
                    v_bias(b, t)
                split(3)
                routing_starts()
                ctx_lo(b, 0)
                dve.wait_ge(s["x_rest"], 16)
            else:
                ctx_lo(b, 0)
                copy_pos(b - 1)
                gated_mul(b - 1, 0)
                gated_mul(b - 1, 1)
                gated_lo(b - 1, 0)
                v_bias(b, 0)
                gated_mul(b - 1, 2)
                gated_lo(b - 1, 1)
                v_bias(b, 1)
                gated_mul(b - 1, 3)
                gated_lo(b - 1, 2)
                gated_lo(b - 1, 3)
                v_bias(b, 2)
                v_bias(b, 3)
                ctx_lo(b, 1)
                for t in range(T):
                    residual(b - 1, t)
                ctx_lo(b, 2)
                for t in range(T):
                    second_stats(b - 1, t)
                for t in range(T):
                    aggregate(2, t, "x2_stat", T * b, "x2_aggr")
            if not last:
                first_stats(b + 1)
            if first:
                for k in range(1, K):
                    ctx_lo(b, k)
            else:
                ctx_lo(b, 3)
                dve.wait_ge(s["rs2"], 2 * b)
                for t in range(T):
                    second_norm(b - 1, t)
            if not last:
                first_norm(b + 1)
            dve.wait_ge(s["kv_mm"], b + 1)
            dve.wait_ge(s["pool_const"], 7)
            dve.tensor_tensor(kvm[:].rearrange("p k e -> p (k e)"), kv_ps[:, :],
                              head_mask[:].rearrange("p k e -> p (k e)"), ALU.mult).then_inc(s["kv_evac"], 1)
            if not last:
                first_norm_lo(b + 1)
            if first:
                routing_positions()
            for t in range(T):
                wait_apart(dve, "o_copy", T * b + t + 1)
                tile_stats(1, t, on[:, t], "o_stat")
            for t in range(T):
                aggregate(1, t, "o_stat", T * b + T, "o_aggr")

        def signs_of(g, j):
            dve.wait_ge(s[f"unit_in{j}"], 16 * (g + 1))
            if not (isinstance(g, int) and g == 0):
                dve.wait_ge(s["unit_mm"], T * (3 * g + j - 2))
            dve.tensor_scalar(signs[:, j, 0], unit_slot[j], thr[:, 0, j:j + 1], None, ALU.is_gt).then_inc(s["sign_a"], 1)
            dve.tensor_scalar(signs[:, j, 1], unit_slot[j], thr[:, 1, j:j + 1], -1.0, ALU.is_lt,
                              ALU.mult).then_inc(s["sign_b"], 1)

        batch(0, True, False)
        with dve.Fori(1, B - 1) as b:
            batch(b, False, False)
        batch(B - 1, False, True)

        dve.wait_ge(s["abs_done"], 3 * B)
        dve.tensor_reduce(abssum[:, :], absacc[:, :, :], AX.X, ALU.add).then_inc(s["scale_step"], 1)
        head_norm(B - 1)
        dve.wait_ge(s["abs_mm"], 1)
        dve.tensor_scalar(qs[:, :], prep[:, 0:3], 1.0 / (FF * D), Q_EPS, ALU.mult, ALU.add).then_inc(s["scale_step"], 1)
        dve.wait_ge(s["scale_step"], 2)
        dve.tensor_scalar(thr[:, 0], qs[:, :], 0.5, None, ALU.mult).then_inc(s["scale_step"], 1)
        dve.tensor_scalar(thr[:, 1], qs[:, :], -0.5, None, ALU.mult).then_inc(s["scale_step"], 1)
        dve.tensor_tensor(hk[:, 1:2], qs[:, 0:1], qs[:, 1:2], ALU.mult).then_inc(s["scale_step"], 1)
        dve.wait_ge(s["scale_step"], 5)
        dve.tensor_scalar(hk[:, 1:2], hk[:, 1:2], qs[:, 2:3], HID_SCALE, ALU.mult, ALU.mult).then_inc(s["scale_step"], 1)
        dve.reciprocal(hk[:, 0:1], qs[:, 0:1]).then_inc(s["scale_step"], 1)
        dve.wait_ge(s["scale_step"], 7)
        dve.tensor_scalar(hk[:, 0:1], hk[:, 0:1], 1.0 / HID_SCALE, None, ALU.mult).then_inc(s["scale_step"], 1)
        dve.wait_ge(s["scale_step"], 8)
        copy_pos(B - 1)
        gated_mul(B - 1, 0)
        for k in range(1, K):
            gated_mul(B - 1, k)
            gated_lo(B - 1, k - 1)
        gated_lo(B - 1, K - 1)
        signs_of(0, 0)
        signs_of(0, 1)

        def last_sum(t):
            residual(B - 1, t)
            second_stats(B - 1, t)
            aggregate(2, t, "x2_stat", T * (B - 1) + t + 1, "x2_aggr")

        def last_norm(t):
            dve.wait_ge(s["rs2_last"], 2 * t + 2)
            second_norm(B - 1, t)

        last_sum(0)
        for t in range(1, T):
            last_sum(t)
            last_norm(t - 1)
        last_norm(T - 1)
        signs_of(0, 2)
        signs_of(1, 0)
        signs_of(1, 1)

        def xs_lo(i):
            dve.wait_ge(s["xs_hi"], i + 1)
            dve.tensor_tensor(xsT[:, 1], tx_ps[:, :], xsT[:, 0], ALU.subtract).then_inc(s["xs_lo"], 1)

        def y_copy(i, slot, uses):
            dve.wait_ge(s["y_mm"], i + 1)
            dve.wait_ge(s[f"ys_out{slot}"], 16 * uses)
            dve.tensor_scalar(ys_slot[slot], y_ps[:, :], CTX_SCALE ** -2, None, ALU.mult).then_inc(s["y_evac"], 1)

        def tile_step(i, quant, prev_slot, prev_uses):
            if quant is not None:
                signs_of(*quant)
            dve.wait_ge(s["z_act"], i + 1)
            dve.wait_ge(s["h_hi"], i)
            dve.tensor_tensor(h32, z_ps[:, :], sil, ALU.mult).then_inc(s["h_mul"], 1)
            xs_lo(i + 1)
            if prev_slot is not None:
                y_copy(i - 1, prev_slot, prev_uses)
            dve.wait_ge(s["h_hi"], i + 1)
            dve.tensor_tensor(hT[:, 1], th_ps[:, :], hT[:, 0], ALU.subtract).then_inc(s["h_lo"], 1)

        xs_lo(0)
        tile_step(0, (1, 2), None, None)
        for g in range(2):
            for j in range(3):
                tile_step(3 * g + j + 1, (g + 2, j), j, g)
        with dve.Fori(2, 6) as g:
            for j in range(3):
                tile_step(3 * g + j + 1, None, j, g)
        dve.wait_ge(s["scattered"], 16 * NT)
        dve.tensor_copy(pos_now[:, :], pos[:, 0:T]).then_inc(s["pos3_copied"], 1)
        y_copy(SLOTS - 1, 0, 6)

        def x3_lo(b, t, bank=t3_ps):
            dve.wait_ge(s["x3_hi"], T * b + t + 1)
            cut = bass.ds(t * P, P)
            hi = x3T[:, bass.ds(b, 1), 0, :, cut].rearrange("p a k s -> p (a k) s")
            lo = x3T[:, bass.ds(b, 1), 1, :, cut].rearrange("p a k s -> p (a k) s")
            dve.tensor_tensor(lo, bank[:, :].rearrange("p (k s) -> p k s", k=K), hi, ALU.subtract).then_inc(s["x3_lo"], 1)

        def sum3_tile(t):
            dve.wait_ge(s[f"y_in_first{t}"], 16)
            dve.tensor_tensor(x_tile(t), n2[:, t], x_tile(t), ALU.add).then_inc(s["y_added"], 1)
            wait_apart(dve, "y_added", t + 1)
            tile_stats(0, t, x_tile(t), "x3_stat")
            aggregate(0, t, "x3_stat", t + 1, "x3_aggr")

        def norm3_tile(t):
            dve.wait_ge(s["rs3_first"], 2 * t + 2)
            normalise(0, nrm[:, t], x_tile(t), t, "x3_norm")

        sum3_tile(0)
        sum3_tile(1)
        norm3_tile(0)
        sum3_tile(2)
        norm3_tile(1)
        x3_lo(0, 0, ps[0])
        sum3_tile(3)
        norm3_tile(2)
        x3_lo(0, 1, ps[1])
        norm3_tile(3)
        dve.tensor_copy(pos_now[:, 0:1], pos[:, T:T + 1]).then_inc(s["pos3_copied"], 1)
        for t in (2, 3):
            x3_lo(0, t, ps[t])

        def x3_sum(b, t):
            i = T * b + t
            dve.wait_ge(s["y_in"], (i - T) * 16 + 16)
            dve.tensor_tensor(x_tile(i), n2[:, 0], x_tile(i), ALU.add).then_inc(s["y_added"], 1)
            wait_apart(dve, "y_added", i + 1)
            dve.bn_stats(st[0][:, 0], x_tile(i)).then_inc(s["x3_stat"], 1)
            wait_apart(dve, "x3_stat", i + 1)
            dve.bn_aggr(mv[0][:, 0], st[0][:, 0]).then_inc(s["x3_aggr"], 1)

        def x3_normalise(b, t):
            i = T * b + t
            dve.wait_ge(s["rs3"], 2 * (i - T) + 2)
            dve.wait_ge(s["t3_mm"], i)
            normalise(0, nrm[:, 0], x_tile(i), 0, "x3_norm")

        def next_pos(i):
            dve.tensor_copy(pos_now[:, 0:1], pos[:, bass.ds(i, 1)]).then_inc(s["pos3_copied"], 1)

        def finish(b):
            dve.wait_ge(s["down_mm"], C * b + C)
            for t in range(T):
                dve.wait_ge(s[f"out_done{t}"], 16 * b)
                dve.scalar_tensor_tensor(out=out_slot[t], in0=ffy_ps[t][:, :], scalar=hk[:, 1:2],
                                         in1=x_tile(T * b + t), op0=ALU.mult, op1=ALU.add).then_inc(s["out_made"], 1)

        def group(b, t, begins, first, nxt, more):
            for cc in range(4):
                cf = C * b + 4 * t + cc
                if begins and cc == 1 and not first:
                    finish(b - 1)
                if nxt and cc == 1:
                    x3_sum(b + 1, t)
                    if more:
                        next_pos(T * (b + 1) + t + 1)
                if nxt and cc == 2:
                    x3_normalise(b + 1, t)
                dve.wait_ge(s["up_act"], cf + 1)
                dve.wait_ge(s["gate_mm"], cf + 1)
                dve.wait_ge(s["hid_hi"], cf)
                dve.wait_ge(s["hid_lo"], cf)
                dve.scalar_tensor_tensor(out=h32, in0=sil, scalar=hk[:, 0:1], in1=gate_ps[:, :], op0=ALU.mult,
                                         op1=ALU.mult).then_inc(s["hid_mul"], 1)
                dve.wait_ge(s["hid_hi"], cf + 1)
                dve.tensor_tensor(hid[:, cc % 2, 1], h32, hid[:, cc % 2, 0], ALU.subtract).then_inc(s["hid_lo"], 1)
                if nxt and cc == 3:
                    x3_lo(b + 1, t)

        def batch3(b, first, nxt):
            group(b, 0, True, first, nxt, True)
            with dve.Fori(1, T) as t:
                group(b, t, False, False, nxt, True)

        batch3(0, True, True)
        with dve.Fori(1, B - 1) as b:
            batch3(b, False, True)
        batch3(B - 1, False, False)
        finish(B - 1)

    @block.tensor
    def _(pe):
        def transposes(dst, src, m=None):
            for i in range(4):
                mm = pe.transpose(dst[:, i * P:(i + 1) * P], src(i), ident[:, :])
            return mm

        def product(dst, lhs, rhs):
            n = 0
            for k in range(K):
                for i, j in PARTS:
                    mm = pe.matmul(dst, lhs(i, j, k), rhs(i, j, k), start=(n == 0), stop=(n == 3 * K - 1))
                    n += 1
            return mm

        def first_norm(b1):
            for t in range(T):
                pe.wait_ge(s["x_norm"], T * b1 + t + 1)
                if t >= 2:
                    pe.wait_ge(s["x_lo"], T * b1 + t - 1)
                transposes(tr[t % 2], lambda k: nrm[:, t, k * P:(k + 1) * P]).then_inc(s["t1_mm"], 1)

        def ctx_part(b, k):
            pe.wait_ge(s["ctx_lo"], 4 * b + k)
            transposes(prep, lambda r: stage[:, 0, r, k * P:(k + 1) * P]).then_inc(s["ctx_mm"], 1)

        def head_norm(b, last):
            pe.wait_ge(s["o_norm"], T * b + T)
            for k in range(K):
                if k < 2:
                    if last:
                        pe.wait_ge(s["k_copy"], T * b + 3 + k)
                    else:
                        pe.wait_ge(s["x_lo"], T * (b + 1) + 3 + k)
                else:
                    pe.wait_ge(s["n_aff"], K * b + k - 1)
                transposes(tr[k % 2], lambda t: on[:, t, k * P:(k + 1) * P]).then_inc(s["tn_mm"], 1)

        def project(b, bank_free):
            pe.wait_ge(s["w_lo"], 4)
            pe.wait_ge(s["a_lo"], K * b + K)
            for t in range(T):
                if t < 2:
                    if bank_free is not None:
                        pe.wait_ge(s["v_bias"], bank_free + t)
                else:
                    pe.wait_ge(s["x1_done"], T * b + t - 1)
                cut = slice(t * P, (t + 1) * P)
                product(acc[t % 2][:, :], lambda i, j, k: aT[:, i, k, cut],
                        lambda i, j, k: w_att[:, 3, j, k]).then_inc(s["wo_mm"], 1)

        def batch(b, first, last):
            pe.wait_ge(s["x_lo"], T * b + T)
            pe.wait_ge(s["w_lo"], 1)
            for m in range(K):
                if m < 2:
                    if not first:
                        pe.wait_ge(s["u_act"], K * (b - 1) + 3 + m)
                else:
                    pe.wait_ge(s["q_elu"], K * b + m - 1)
                product(acc[m % 2][:, :], lambda i, j, k: w_att[:, 0, j, k, m * P:(m + 1) * P],
                        lambda i, j, k: xT[:, i, k]).then_inc(s["q_mm"], 1)
            if first:
                routing_sums()
            else:
                pe.wait_ge(s["stage_in0"], 32 * b + 16)
                ctx_part(b, 0)
                head_norm(b - 1, False)
            pe.wait_ge(s["w_lo"], 2)
            for t in range(T):
                if t < 2:
                    pe.wait_ge(s["q_elu"], K * b + 3 + t)
                else:
                    pe.wait_ge(s["v_bias"], T * b + t - 1)
                cut = slice(t * P, (t + 1) * P)
                product(acc[t % 2][:, :], lambda i, j, k: xT[:, i, k, cut],
                        lambda i, j, k: w_att[:, 1, j, k]).then_inc(s["v_mm"], 1)
            if not first:
                ctx_part(b, 1)
                project(b - 1, T * b + 3)
                ctx_part(b, 2)
            for t in range(T):
                if t < 2:
                    if first:
                        pe.wait_ge(s["x_lo"], 3 + t)
                    else:
                        pe.wait_ge(s["n_aff"], K * (b - 1) + 3 + t)
                else:
                    pe.wait_ge(s["k_copy"], T * b + t - 1)
                transposes(tr[t % 2], lambda k: qT[:, k, t * P:(t + 1) * P]).then_inc(s["tk_mm"], 1)
            if first:
                pe.wait_ge(s["stage_in0"], 16)
                ctx_part(b, 0)
            else:
                ctx_part(b, 3)
            pe.wait_ge(s["w_lo"], 3)
            for m in range(K):
                if m < 2:
                    if first:
                        pe.wait_ge(s["v_bias"], 3 + m)
                    else:
                        pe.wait_ge(s["x1_done"], T * (b - 1) + 3 + m)
                else:
                    pe.wait_ge(s["u_act"], K * b + m - 1)
                product(acc[m % 2][:, :], lambda i, j, k: w_att[:, 2, j, k, m * P:(m + 1) * P],
                        lambda i, j, k: xT[:, i, k]).then_inc(s["u_mm"], 1)
                if first and m < 3:
                    ctx_part(b, m + 1)
            pe.wait_ge(s["k_copy"], T * b + T)
            pe.wait_ge(s["v_act"], T * b + T)
            pe.wait_ge(s["kv_evac"], b)
            if first:
                pe.wait_ge(s["route_read"], 1)
            for m in range(K):
                cut = slice(m * P, (m + 1) * P)
                for t in range(T):
                    mm = pe.matmul(kv_ps[:, cut], kk[:, t, cut], vv[:, t, cut], start=(t == 0), stop=(t == T - 1))
            mm.then_inc(s["kv_mm"], 1)
            if not last:
                first_norm(b + 1)
            pe.wait_ge(s["kv_evac"], b + 1)
            for t in range(T):
                if t < 2:
                    if not first:
                        pe.wait_ge(s["o_copy"], T * (b - 1) + 3 + t)
                else:
                    pe.wait_ge(s["o_copy"], T * b + t - 1)
                for k in range(K):
                    cut = slice(k * P, (k + 1) * P)
                    mm = pe.matmul(o_ps[t % 2][:, cut], qT[:, k, t * P:(t + 1) * P], kvm[:, k], start=True, stop=True)
                mm.then_inc(s["o_mm"], 1)

        def routing_sums():
            pe.wait_ge(s["route_step"], E + 3)
            pe.wait_ge(s["pool_const"], 3)
            flat = member[:, :, :].rearrange("p e c -> p (e c)")
            n = E * NT
            pe.matmul(kv_ps[:, 0:n], ones[:, :], flat, start=True, stop=True).then_inc(s["route_mm"], 1)
            pe.matmul(kv_ps[:, n:2 * n], tri[:, :], flat, start=True, stop=True).then_inc(s["route_mm"], 1)

        def unit_transposes(g, j):
            pe.wait_ge(s["sign_b"], 3 * g + j + 1)
            for r in range(T):
                if not (isinstance(g, int) and g == 0 and j == 0):
                    pe.wait_ge(s["unit_copy"], T * (3 * g + j - 1) + r + 1)
                for q in range(T):
                    cut = slice(q * P, (q + 1) * P)
                    for h in range(2):
                        mm = pe.matmul(q_ps[r][:, cut], signs[:, j, h, r, cut], ident_b[:, :],
                                         start=(h == 0), stop=(h == 1))
                mm.then_inc(s["unit_mm"], 1)

        pe.wait_ge(s["ident_made"], 1)
        first_norm(0)
        batch(0, True, False)
        with pe.Fori(1, B - 1) as b:
            batch(b, False, False)
        batch(B - 1, False, True)
        pe.wait_ge(s["scale_step"], 1)
        pe.wait_ge(s["ctx_lo"], 4 * B)
        pe.matmul(prep[:, 0:3], ones[:, :], abssum[:, :], start=True, stop=True).then_inc(s["abs_mm"], 1)
        head_norm(B - 1, True)
        project(B - 1, None)
        pe.wait_ge(s["scale_step"], 2)
        pe.wait_ge(s["o_copy"], NT)
        for g, j in ((0, 0), (0, 1), (0, 2), (1, 0), (1, 1)):
            unit_transposes(g, j)

        def xs_transpose(i, slot, slot_count):
            pe.wait_ge(s[f"xs_in{slot}"], 16 * slot_count)
            pe.wait_ge(s["xs_lo"], i)
            transposes(tx_ps, lambda k: xs_slot[slot][:, k * P:(k + 1) * P]).then_inc(s["tx_mm"], 1)

        def expert(i):
            return pe.value_load(tile_expert[0:1, bass.ds(i, 1)], min_val=0, max_val=E - 1)

        def moe(dst, lhs, e):
            return product(dst, lambda i, j, k: lhs[:, i, k * P:(k + 1) * P],
                           lambda i, j, k: w_moe[:, bass.ds(e, 1), j, k].rearrange("p a d -> p (a d)"))

        def second(i):
            e = expert(i)
            pe.wait_ge(s["h_lo"], i + 1)
            pe.wait_ge(s["y_evac"], i)
            moe(y_ps[:, :], hT, e).then_inc(s["y_mm"], 1)

        def tile_step(i, quant, slot, slot_count, first):
            e = expert(i)
            pe.wait_ge(s["xs_lo"], i + 1)
            pe.wait_ge(s["h_mul"], i)
            moe(z_ps[:, :], xsT, e).then_inc(s["z_mm"], 1)
            xs_transpose(i + 1, slot, slot_count)
            if not first:
                second(i - 1)
            if quant is not None:
                unit_transposes(*quant)
            pe.wait_ge(s["h_mul"], i + 1)
            pe.wait_ge(s["h_lo"], i)
            transposes(th_ps, lambda k: h32[:, k * P:(k + 1) * P]).then_inc(s["th_mm"], 1)

        xs_transpose(0, 0, 1)
        tile_step(0, (1, 2), 1, 1, True)
        with pe.Fori(0, 2) as g:
            for j in range(3):
                tile_step(3 * g + j + 1, (g + 2, j), (j + 2) % 3, g + 1 + (j + 2) // 3, False)
        with pe.Fori(2, 6) as g:
            for j in range(3):
                tile_step(3 * g + j + 1, None, (j + 2) % 3, g + 1 + (j + 2) // 3, False)
        second(SLOTS - 1)

        def x3_transpose(i, t, bank):
            pe.wait_ge(s["x3_norm"], i + 1)
            if bank is t3_ps:
                pe.wait_ge(s["x3_lo"], i)
            transposes(bank, lambda k: nrm[:, t, k * P:(k + 1) * P]).then_inc(s["t3_mm"], 1)

        def two_pass(dst, w, cf_c, b):
            for k in range(K):
                for i in range(2):
                    mm = pe.matmul(dst, w[:, bass.ds(cf_c, 1), k * P:(k + 1) * P].rearrange("p a n -> p (a n)"),
                                     x3T[:, bass.ds(b, 1), i, k].rearrange("p a s -> p (a s)"),
                                     start=(k == 0 and i == 0), stop=(k == K - 1 and i == 1))
            return mm

        def down(cf, c, parity, start, stop):
            pe.wait_ge(s["hid_lo"], cf + 1)
            for t in range(T):
                for i in range(2):
                    mm = pe.matmul(ffy_ps[t][:, :], hid[:, parity, i, t * P:(t + 1) * P],
                                     tern[2][:, bass.ds(c, 1)].rearrange("p a n -> p (a n)"),
                                     start=(start and i == 0), stop=(stop and i == 1))
            mm.then_inc(s["down_mm"], 1)

        def group(b, t, begins, first, nxt):
            for cc in range(4):
                c = 4 * t + cc
                cf = C * b + c
                begin = first and cc == 0
                if not begin:
                    pe.wait_ge(s["up_act"], cf)
                two_pass(up_ps[:, :], tern[0], c, b).then_inc(s["up_mm"], 1)
                if not begin:
                    pe.wait_ge(s["hid_mul"], cf)
                two_pass(gate_ps[:, :], tern[1], c, b).then_inc(s["gate_mm"], 1)
                if begins and cc == 0:
                    if not first:
                        down(cf - 1, C - 1, 1, False, True)
                else:
                    if begins and cc == 1 and not first:
                        pe.wait_ge(s["out_made"], T * b)
                    down(cf - 1, c - 1, (cc - 1) % 2, begins and cc == 1, False)
                if nxt and cc == 2:
                    x3_transpose((b + 1) * T + t, 0, t3_ps)

        for t in range(T):
            x3_transpose(t, t, ps[t])
        pe.wait_ge(s["unit_copy"], 12 * T)

        def batch3(b, first, nxt):
            pe.wait_ge(s["x3_lo"], T * b + T)
            group(b, 0, True, first, nxt)
            with pe.Fori(1, T) as t:
                group(b, t, False, False, nxt)

        batch3(0, True, True)
        with pe.Fori(1, B - 1) as b:
            batch3(b, False, True)
        batch3(B - 1, False, False)
        down(C * B - 1, C - 1, 1, False, True)

    es.close()


_INS = ['x', 'itok_BxS_13_99985', 'ctx_2048', 'L0_attn_Wqk', 'L0_attn_bqk', 'L0_attn_Wv', 'L0_attn_bv', 'L0_attn_Wu',
        'L0_attn_bu', 'L0_attn_Wo', 'L0_attn_bo', 'L0_attn_ln_g', 'L0_attn_ln_b', 'L0_ffn_W_up', 'L0_ffn_W_gate',
        'L0_ffn_W_down']


def kernel(**inputs):
    import concourse.bacc as _bacc
    from concourse.bass_utils import run_bass_kernel_spmd as _run

    nc = _bacc.Bacc("TRN2", target_bir_lowering=False, num_devices=1)
    arrays, args = {}, []
    for name in _INS:
        a = np.ascontiguousarray(inputs[name])
        arrays[f"in_{name}_dram"] = a
        args.append(nc.dram_tensor(f"in_{name}_dram", a.shape, mybir.dt.from_np(a.dtype), kind="ExternalInput").ap())
    args.append(nc.dram_tensor("out_0_dram", (B, S, D), F32, kind="ExternalOutput").ap())
    decoder(nc, *args)
    r = _run(nc, [arrays], core_ids=[0])
    return r.results[0]["out_0_dram"]
```

```python
from contextlib import ExitStack

import numpy as np

import concourse.bass as bass
from concourse import mybir

ALU = mybir.AluOpType
ACT = mybir.ActivationFunctionType
AX = mybir.AxisListType
F32 = mybir.dt.float32
F16 = mybir.dt.float16
BF16 = mybir.dt.bfloat16
I32 = mybir.dt.int32

P = 128
B, S, D = 4, 512, 512
FF = 2048
K = D // P
T = S // P
NT = B * T
HD = 32
E = 4
VOCAB = 25000
SLOTS = NT + E - 1
C = FF // P
CTX_SCALE = 256.0
HID_SCALE = 8.0
LN_EPS = 1e-5
Q_EPS = 1e-8
PARTS = ((0, 0), (1, 0), (0, 1))


def decoder(nc, x, itok, ctx_w, Wqk, bqk, Wv, bv, Wu, bu, Wo, bo, ln_g, ln_b, W_up, W_gate, W_down, out):
    es = ExitStack()

    def sb(name, shape, dt=F32):
        return es.enter_context(nc.sbuf_tensor(name, shape, dt))

    def sem(name):
        return es.enter_context(nc.semaphore(name))

    x_v = x.rearrange("b (t p) d -> p (b t) d", p=P)
    out_v = out.rearrange("b (t p) d -> p (b t) d", p=P)
    tok_v = itok.rearrange("b (t p) -> p (b t)", p=P)
    ctx_v = ctx_w.rearrange("e (r p) d -> p e r d", p=P)
    att_v = [w.rearrange("(k p) n -> p k n", p=P) for w in (Wqk, Wv, Wu, Wo)]
    unit_v = [W_up.rearrange("(g r p) d -> p g r d", r=T, p=P),
              W_gate.rearrange("(g r p) d -> p g r d", r=T, p=P),
              W_down.rearrange("(g p) (r d) -> p g r d", p=P, r=T)]
    column = lambda v: v.rearrange("(k p) -> p k", p=P)
    xs_dram = nc.dram_tensor("sorted_tokens", ((SLOTS + 1) * P, D), F32, kind="Internal").ap()
    ys_dram = nc.dram_tensor("sorted_outputs", (SLOTS * P, D), F32, kind="Internal").ap()
    xs_v = xs_dram.rearrange("(c p) d -> p c d", p=P)
    ys_v = ys_dram.rearrange("(c p) d -> p c d", p=P)

    resid = sb("resid", [P, NT, D])
    w_att = sb("w_att", [P, 4, 2, K, D], F16)
    w_moe = sb("w_moe", [P, E, 2, K, D], F16)
    region = sb("region", [P, 6, T, D])
    stage = sb("stage", [P, 2, T, D])
    nrm = sb("nrm", [P, T, D])
    n2 = sb("n2", [P, T, D])
    tmp = sb("tmp", [P, 2, D])
    tmpA = sb("tmpA", [P, 2, D])
    a32 = sb("a32", [P, 2, D])
    kvm = sb("kvm", [P, K, P])
    xT = sb("xT", [P, 2, K, S], F16)
    bv_bc = sb("bv_bc", [P, D])
    bo_bc = sb("bo_bc", [P, D])
    head_mask = sb("head_mask", [P, K, P])
    cols = sb("cols", [P, 4, K])
    ident = sb("ident", [P, P])
    ident_b = sb("ident_b", [P, P], BF16)
    ones = sb("ones", [P, P])
    tri = sb("tri", [P, P])
    halfs = sb("halfs", [P, T])
    st = [sb(f"st{i}", [P, T, 6]) for i in range(3)]
    mv = [sb(f"mv{i}", [P, T, 2]) for i in range(3)]
    ve = [sb(f"ve{i}", [P, T]) for i in range(3)]
    rs = [sb(f"rs{i}", [P, T]) for i in range(3)]
    absacc = sb("absacc", [P, 3, B])
    abssum = sb("abssum", [P, 3])
    qs = sb("qs", [P, 3])
    thr = sb("thr", [P, 2, 3])
    hk = sb("hk", [P, 2])
    tok = sb("tok", [P, NT], I32)
    tokf = sb("tokf", [P, NT])
    pad_i = sb("pad_i", [P, 2, E], I32)
    pad_f = sb("pad_f", [P, E])
    base = sb("base", [P, E])
    pos_f = sb("pos_f", [P, NT])
    pos = sb("pos", [P, NT + 1], I32)
    pos_now = sb("pos_now", [P, T], I32)
    starts_i = sb("starts_i", [1, SLOTS], I32)
    starts = sb("starts", [1, SLOTS])
    te_f = sb("te_f", [1, E, SLOTS])
    tile_expert = sb("tile_expert", [1, SLOTS], I32)

    rt = region[:, 5, 0, 0:(3 * E + 1 + E) * NT].rearrange("p (e c) -> p e c", c=NT)
    ge, member, before = rt[:, 0:E + 1], rt[:, E + 1:2 * E + 1], rt[:, 2 * E + 1:3 * E + 1]
    scan = region[:, 5, 1, 0:2 * E * NT].rearrange("p (i e c) -> p i e c", i=2, e=E)
    qT, kk, vv, uT, on = [region[:, i] for i in range(5)]
    aT = region[:, 5].rearrange("p a b -> p (a b)").bitcast(F16).rearrange("p (h k s) -> p h k s", h=2, k=K)
    tern = [region[:, 2 * i:2 * i + 2].rearrange("p a b c -> p (a b c)").bitcast(BF16)
            .rearrange("p (c n) -> p c n", c=C) for i in range(3)]
    signs = w_att[:].rearrange("p a b c d -> p (a b c d)")[:, 0:6 * FF].bitcast(BF16).rearrange(
        "p (j s r d) -> p j s r d", j=3, s=2, r=T)
    x3T = w_att
    att_slot = [stage[:, 0], stage[:, 1], on, n2[:, :, :]]
    out_slot = [stage[:, 0, t] for t in range(T)]
    unit_slot = [stage[:, 0], stage[:, 1], nrm[:, :, :]]
    xs_slot = [n2[:, i] for i in range(3)]
    ys_slot = [n2[:, 3], a32[:, 0], a32[:, 1]]
    sil, h32 = tmp[:, 0], tmp[:, 1]
    tA = tmpA[:].rearrange("p a b -> p (a b)").bitcast(F16).rearrange("p (i h n) -> p i h n", i=2, h=2)
    xsT, hT = tA[:, 0], tA[:, 1]
    hid = tA

    ps = [es.enter_context(nc.psum_tensor(f"bank{i}", [P, 512], F32)) for i in range(8)]
    acc, tr, kv_ps, o_ps, prep = ps[0:2], ps[2:4], ps[4], ps[5:7], ps[7]
    z_ps, y_ps, tx_ps, th_ps, q_ps = ps[0], ps[1], ps[2], ps[3], ps[4:8]
    ffy_ps, up_ps, gate_ps, t3_ps = ps[0:4], ps[4], ps[5], ps[6]

    names = """x_first0 x_first1 x_first2 x_first3 x_rest cols_in rows_in tok_in att_in0 att_in1 att_in2
        att_in3 stage_in0 stage_in1 zeroed scattered xs_in0 xs_in1 xs_in2 unit_in0 unit_in1 unit_in2
        ys_out0 ys_out1 ys_out2 ys_out_last y_in y_in_first0 y_in_first1 y_in_first2 y_in_first3
        out_done0 out_done1 out_done2 out_done3
        ident_made pool_const zero_src starts_made bias_added rs1_first rs1 rs_o rs_o_last rs2 rs2_last rs3 rs3_first
        w_hi w_lo ctx_mm ctx_hi ctx_lo abs_done abs_mm scale_step
        route_step route_mm route_read route_ready
        x_stat x_aggr x_norm t1_mm x_hi x_lo
        q_mm q_exp q_clip q_elu tn_mm n_aff a_mul a_hi a_lo v_mm v_bias v_act wo_mm x1_done
        x2_stat x2_aggr x2_norm tk_mm k_copy u_mm u_act kv_mm kv_evac o_mm o_copy o_stat o_aggr o_norm
        tx_mm xs_hi xs_lo z_mm z_act h_mul th_mm h_hi h_lo y_mm y_evac sign_a sign_b unit_mm unit_copy
        y_added x3_stat x3_aggr x3_norm t3_mm x3_hi x3_lo pos3_copied
        up_mm gate_mm up_act hid_mul hid_hi hid_lo down_mm down_last out_made""".split()
    s = {n: sem(n) for n in names}

    def wait_apart(eng, name, value):
        if not isinstance(value, int):
            eng.lower_val(value)
        eng.wait_ge(s["zero_src"], 1)
        eng.wait_ge(s[name], value)

    block = es.enter_context(nc.Block())

    @block.sync
    def _(sp):
        for t in range(T):
            sp.dma_start(resid[:, t], x_v[:, t]).then_inc(s[f"x_first{t}"], 16)
        sp.dma_start(att_slot[0], att_v[0]).then_inc(s["att_in0"], 16)
        for i, v in enumerate((bqk, bu, ln_g, ln_b)):
            sp.dma_start(cols[:, i], column(v), allow_slow_non_contiguous=True).then_inc(s["cols_in"], 16)
        sp.dma_start(tok[:, :], tok_v, allow_slow_non_contiguous=True).then_inc(s["tok_in"], 16)
        for m in (1, 2, 3):
            sp.dma_start(att_slot[m], att_v[m]).then_inc(s[f"att_in{m}"], 16)
        sp.dma_start(bv_bc[:, :], bv.partition_broadcast(P)).then_inc(s["rows_in"], 16)
        sp.dma_start(bo_bc[:, :], bo.partition_broadcast(P)).then_inc(s["rows_in"], 16)
        sp.dma_start(resid[:, T:NT], x_v[:, T:NT]).then_inc(s["x_rest"], 16)

        def expert_weights(b):
            sp.dma_start(stage[:, 0], ctx_v[:, bass.ds(b, 1)].rearrange("p a r d -> p (a r) d")).then_inc(
                s["stage_in0"], 16)

        def summed_unit(b, j, slot):
            sp.dma_start(stage[:, slot], unit_v[j][:, bass.ds(b, 1)].rearrange("p a r d -> p (a r) d")).then_inc(
                s[f"stage_in{slot}"], 16)

        def weights(b, first):
            if first:
                sp.wait_ge(s["w_lo"], 1)
                expert_weights(b)
                sp.wait_ge(s["w_lo"], 2)
                summed_unit(b, 0, 1)
                sp.wait_ge(s["zero_src"], 1)
                with sp.Fori(0, (SLOTS + 1) // 2) as i:
                    sp.dma_start(xs_v[:, bass.ds(2 * i, 2)], a32[:, :, :]).then_inc(s["zeroed"], 16)
            else:
                sp.wait_ge(s["abs_done"], 3 * b - 1)
                expert_weights(b)
                sp.wait_ge(s["abs_done"], 3 * b)
                summed_unit(b, 0, 1)
            sp.wait_ge(s["ctx_mm"], 4 * b + 4)
            summed_unit(b, 1, 0)
            sp.wait_ge(s["abs_done"], 3 * b + 1)
            summed_unit(b, 2, 1)

        weights(0, True)
        with sp.Fori(1, B) as b:
            weights(b, False)

        def unit(g, j):
            sp.dma_start(unit_slot[j], unit_v[j][:, bass.ds(g, 1)].rearrange("p a r d -> p (a r) d")).then_inc(
                s[f"unit_in{j}"], 16)

        def sorted_tile(i, slot):
            sp.dma_start(xs_slot[slot], xs_v[:, bass.ds(i, 1)].rearrange("p a d -> p (a d)")).then_inc(
                s[f"xs_in{slot}"], 16)

        sp.wait_ge(s["abs_done"], 3 * B - 1)
        unit(0, 0)
        sp.wait_ge(s["abs_done"], 3 * B)
        unit(0, 1)
        sp.wait_ge(s["t1_mm"], T * B)
        unit(0, 2)
        sp.wait_ge(s["sign_b"], 1)
        unit(1, 0)
        sp.wait_ge(s["scattered"], 16 * NT)
        sorted_tile(0, 0)
        for j in (1, 2):
            sp.wait_ge(s["sign_b"], j + 1)
            unit(1, j)
            sorted_tile(j, j)
        with sp.Fori(2, 4) as g:
            for j in range(3):
                sp.wait_ge(s["sign_b"], 3 * (g - 1) + j + 1)
                unit(g, j)
                sp.wait_ge(s["tx_mm"], 3 * (g - 2) + j + 1)
                sorted_tile(3 * (g - 1) + j, j)
        with sp.Fori(2, 5) as g:
            for j in range(3):
                sp.wait_ge(s["tx_mm"], 3 * g + j + 1)
                sorted_tile(3 * g + j + 3, j)
        for i in (18, 19):
            sp.wait_ge(s["tx_mm"], i - 2)
            sorted_tile(i, i % 3)

        sp.wait_ge(s["y_evac"], SLOTS)
        sp.dma_start(ys_v[:, SLOTS - 1], ys_slot[0]).then_inc(s["ys_out_last"], 16)

        with sp.Fori(0, B) as b:
            for t in range(T):
                sp.wait_ge(s["out_made"], T * b + t + 1)
                sp.dma_start(out_v[:, bass.ds(T * b + t, 1)].rearrange("p a d -> p (a d)"), out_slot[t]).then_inc(
                    s[f"out_done{t}"], 16)
        for t in range(T):
            sp.wait_ge(s[f"out_done{t}"], 16 * B)

    @block.gpsimd
    def _(pool):
        pool.memset(ones[:, :], 1.0).then_inc(s["pool_const"], 1)
        pool.memset(halfs[:, :], -0.5).then_inc(s["pool_const"], 1)
        pool.wait_ge(s["pool_const"], 2)
        pool.affine_select(out=ident[:, :], in_=ones[:, :], compare_op=ALU.is_equal, fill=0.0, base=0,
                           pattern=[[-1, P]], channel_multiplier=1).then_inc(s["ident_made"], 1)
        pool.affine_select(out=tri[:, :], in_=ones[:, :], compare_op=ALU.is_gt, fill=0.0, base=0,
                           pattern=[[1, P]], channel_multiplier=-1).then_inc(s["pool_const"], 1)
        pool.memset(a32[:, :, :], 0.0).then_inc(s["zero_src"], 1)

        def late_constants():
            pool.memset(head_mask[:, :, :], 1.0).then_inc(s["pool_const"], 1)
            pool.wait_ge(s["pool_const"], 4)
            hm = head_mask[:].rearrange("p k (j e) -> p k j e", e=HD)
            pool.affine_select(out=hm, in_=hm, compare_op=ALU.is_ge, fill=0.0, base=0,
                               pattern=[[0, K], [-HD, P // HD], [0, HD]], channel_multiplier=1).then_inc(s["pool_const"], 1)
            pool.wait_ge(s["pool_const"], 5)
            pool.affine_select(out=hm, in_=hm, compare_op=ALU.is_ge, fill=0.0, base=HD - 1,
                               pattern=[[0, K], [HD, P // HD], [0, HD]], channel_multiplier=-1).then_inc(s["pool_const"], 1)
            pool.tensor_copy(ident_b[:, :], ident[:, :]).then_inc(s["pool_const"], 1)
            pool.iota(starts_i[:, :], pattern=[[P, SLOTS]], base=0, channel_multiplier=0).then_inc(s["starts_made"], 1)

        def rsqrt(i, aggr, wait, tiles, done, k):
            wait_apart(pool, aggr, wait)
            pool.tensor_scalar(ve[i][:, tiles], mv[i][:, tiles, 1], LN_EPS, 0.0, ALU.add, ALU.add).then_inc(s[done], 1)
            pool.wait_ge(s[done], 2 * k + 1)
            pool.tensor_tensor(rs[i][:, tiles], ve[i][:, tiles], halfs[:, tiles], ALU.pow).then_inc(s[done], 1)

        def rsqrt_tile(i, aggr, n0, t, done):
            rsqrt(i, aggr, n0 + t + 1, slice(t, t + 1), done, t)

        def scatter(b, t):
            wait_apart(pool, "x2_norm", T * b + t + 1)
            pool.indirect_dma_start(xs_dram, bass.IndirectOffsetOnAxis(ap=pos_now[:, t:t + 1], axis=0),
                                    n2[:, t], None).then_inc(s["scattered"], 16)

        def batch(b, first, last):
            pool.wait_ge(s["x_norm"], T * b + T)
            for t in range(T):
                xt = resid[:, bass.ds(T * b + t, 1)].rearrange("p a d -> p (a d)")
                pool.tensor_tensor(xt, xt, bo_bc[:, :], ALU.add).then_inc(s["bias_added"], 1)
            if not first:
                rsqrt(2, "x2_aggr", T * b, slice(0, T), "rs2", b - 1)
            if not last:
                rsqrt(0, "x_aggr", T * b + 2 * T, slice(0, T), "rs1", b)
            if not first:
                for t in range(T):
                    scatter(b - 1, t)
            if not last:
                rsqrt(1, "o_aggr", T * b + T, slice(0, T), "rs_o", b)

        for t in range(T):
            rsqrt_tile(0, "x_aggr", 0, t, "rs1_first")
        late_constants()
        pool.wait_ge(s["rows_in"], 32)
        batch(0, True, False)
        pool.wait_ge(s["zeroed"], 16 * ((SLOTS + 1) // 2))
        with pool.Fori(1, B - 1) as b:
            batch(b, False, False)
        batch(B - 1, False, True)
        for t in range(T):
            rsqrt_tile(1, "o_aggr", T * (B - 1), t, "rs_o_last")
        rsqrt_tile(2, "x2_aggr", T * (B - 1), 0, "rs2_last")
        for t in range(1, T):
            rsqrt_tile(2, "x2_aggr", T * (B - 1), t, "rs2_last")
            scatter(B - 1, t - 1)
        scatter(B - 1, T - 1)

        def store(i, slot, j):
            pool.wait_ge(s["y_evac"], j)
            pool.dma_start(ys_v[:, bass.ds(i, 1)].rearrange("p a d -> p (a d)"), ys_slot[slot]).then_inc(
                s[f"ys_out{slot}"], 16)

        with pool.Fori(0, 6) as g:
            for j in range(3):
                store(3 * g + j, j, 3 * g + j + 1)

        for slot in range(3):
            pool.wait_ge(s[f"ys_out{slot}"], 16 * 6)
        pool.wait_ge(s["ys_out_last"], 16)

        for t in range(T):
            pool.wait_ge(s["pos3_copied"], 1)
            pool.indirect_dma_start(n2[:, t], None, ys_dram,
                                    bass.IndirectOffsetOnAxis(ap=pos_now[:, t:t + 1], axis=0)).then_inc(
                                        s[f"y_in_first{t}"], 16)
        for t in range(T):
            rsqrt_tile(0, "x3_aggr", 0, t, "rs3_first")
        with pool.Fori(T, NT) as i:
            wait_apart(pool, "pos3_copied", i - T + 2)
            pool.indirect_dma_start(n2[:, 0], None, ys_dram,
                                    bass.IndirectOffsetOnAxis(ap=pos_now[:, 0:1], axis=0)).then_inc(s["y_in"], 16)
            rsqrt(0, "x3_aggr", i + 1, slice(0, 1), "rs3", i - T)

    @block.scalar
    def _(act):
        def first_norm(b1, tiles=range(T)):
            for t in tiles:
                act.wait_ge(s["t1_mm"], T * b1 + t + 1)
                act.activation(xT[:, 0, :, t * P:(t + 1) * P], tr[t % 2].rearrange("p (k s) -> p k s", k=K),
                               ACT.Copy).then_inc(s["x_hi"], 1)

        def split(m):
            act.wait_ge(s[f"att_in{m}"], 16)
            act.activation(w_att[:, m, 0], att_slot[m], ACT.Copy).then_inc(s["w_hi"], 1)

        def ctx_hi(b, k):
            act.wait_ge(s["ctx_mm"], 4 * b + k + 1)
            act.activation(w_moe[:, bass.ds(b, 1), 0, k].rearrange("p a d -> p (a d)"), prep[:, :], ACT.Copy,
                           scale=CTX_SCALE).then_inc(s["ctx_hi"], 1)

        def affine(b, k):
            act.wait_ge(s["tn_mm"], K * b + k + 1)
            if k >= 2:
                act.wait_ge(s["a_mul"], K * b + k - 1)
            act.activation(tmpA[:, k % 2], tr[k % 2][:, :], ACT.Identity, bias=cols[:, 3, k:k + 1],
                           scale=cols[:, 2, k:k + 1]).then_inc(s["n_aff"], 1)

        def gated_hi(b, k):
            act.wait_ge(s["a_mul"], K * b + k + 1)
            act.activation(aT[:, 0, k], a32[:, k % 2], ACT.Copy).then_inc(s["a_hi"], 1)

        def v_act(b, t):
            act.wait_ge(s["v_bias"], T * b + t + 1)
            act.activation(vv[:, t], vv[:, t], ACT.Silu).then_inc(s["v_act"], 1)

        def magnitudes(b, j):
            slot, n = ((1, 1), (0, 2), (1, 2))[j]
            act.wait_ge(s[f"stage_in{slot}"], 32 * b + 16 * n)
            act.activation(stage[:, slot], stage[:, slot], ACT.Abs,
                           accum_out=absacc[:, j, bass.ds(b, 1)]).then_inc(s["abs_done"], 1)

        def batch(b, first, last):
            for m in range(K):
                act.wait_ge(s["q_mm"], K * b + m + 1)
                if not first or m >= 2:
                    act.wait_ge(s["q_elu"], K * b + m - 1)
                act.activation(tmp[:, m % 2], acc[m % 2][:, :], ACT.Exp, bias=cols[:, 0, m:m + 1]).then_inc(s["q_exp"], 1)
            if first:
                split(2)
                for t in range(T):
                    v_act(b, t)
            else:
                ctx_hi(b, 0)
                affine(b - 1, 0)
                affine(b - 1, 1)
                gated_hi(b - 1, 0)
                affine(b - 1, 2)
                gated_hi(b - 1, 1)
                v_act(b, 0)
                affine(b - 1, 3)
                gated_hi(b - 1, 2)
                v_act(b, 1)
                gated_hi(b - 1, 3)
                v_act(b, 2)
                v_act(b, 3)
                ctx_hi(b, 1)
            act.wait_ge(s["kv_mm"], b)
            for t in range(T):
                act.wait_ge(s["tk_mm"], T * b + t + 1)
                act.activation(kk[:, t], tr[t % 2][:, :], ACT.Copy).then_inc(s["k_copy"], 1)
                if not first and t == 1:
                    ctx_hi(b, 2)
            if first:
                ctx_hi(b, 0)
            magnitudes(b, 0)
            act.wait_ge(s["a_mul"], K * b)
            for m in range(K):
                act.wait_ge(s["u_mm"], K * b + m + 1)
                act.activation(uT[:, m], acc[m % 2][:, :], ACT.Silu, bias=cols[:, 1, m:m + 1]).then_inc(s["u_act"], 1)
                if first and m < 3:
                    ctx_hi(b, m + 1)
                elif not first and m == 0:
                    ctx_hi(b, 3)
                if first and m == 0:
                    split(3)
                elif not first and m == 2:
                    magnitudes(b, 1)
            if not last:
                first_norm(b + 1)
            if first:
                magnitudes(b, 1)
            act.wait_ge(s["tn_mm"], K * b)
            for t in range(T):
                act.wait_ge(s["o_mm"], T * b + t + 1)
                act.activation(on[:, t], o_ps[t % 2][:, :], ACT.Copy).then_inc(s["o_copy"], 1)
            magnitudes(b, 2)

        def unit_copies(g, j):
            for r in range(T):
                act.wait_ge(s["unit_mm"], T * (3 * g + j) + r + 1)
                if j < 2:
                    dst, src = tern[j][:, bass.ds(T * g + r, 1)].rearrange("p a n -> p (a n)"), q_ps[r][:, :]
                else:
                    dst, src = tern[j][:, T * r:T * r + T, bass.ds(P * g, P)], q_ps[r].rearrange("p (c d) -> p c d", c=T)
                act.activation(dst, src, ACT.Copy).then_inc(s["unit_copy"], 1)

        first_norm(0, (0, 1))
        split(0)
        first_norm(0, (2, 3))
        split(1)
        act.wait_ge(s["cols_in"], 64)
        batch(0, True, False)
        with act.Fori(1, B - 1) as b:
            batch(b, False, False)
        batch(B - 1, False, True)
        affine(B - 1, 0)
        for k in range(1, K):
            affine(B - 1, k)
            gated_hi(B - 1, k - 1)
        gated_hi(B - 1, K - 1)
        for j in range(3):
            unit_copies(0, j)

        def xs_hi(i):
            act.wait_ge(s["tx_mm"], i + 1)
            act.wait_ge(s["z_mm"], i)
            act.activation(xsT[:, 0], tx_ps[:, :], ACT.Copy).then_inc(s["xs_hi"], 1)

        def tile_step(i, units=()):
            act.wait_ge(s["z_mm"], i + 1)
            act.wait_ge(s["h_mul"], i)
            act.activation(sil, z_ps[:, :], ACT.Silu, scale=1.0 / CTX_SCALE).then_inc(s["z_act"], 1)
            xs_hi(i + 1)
            for g, j in units:
                unit_copies(g, j)
            act.wait_ge(s["th_mm"], i + 1)
            act.wait_ge(s["y_mm"], i)
            act.activation(hT[:, 0], th_ps[:, :], ACT.Copy).then_inc(s["h_hi"], 1)

        xs_hi(0)
        unit_copies(1, 0)
        tile_step(0, ((1, 1), (1, 2)))
        for j in range(3):
            tile_step(j + 1, ((2, j),))
        with act.Fori(4, SLOTS) as i:
            tile_step(i)
        for j in range(3):
            unit_copies(3, j)

        def x3_hi(b, t, bank=t3_ps):
            act.wait_ge(s["t3_mm"], T * b + t + 1)
            act.activation(x3T[:, bass.ds(b, 1), 0, :, bass.ds(t * P, P)].rearrange("p a k s -> p (a k) s"),
                           bank[:, :].rearrange("p (k s) -> p k s", k=K), ACT.Copy).then_inc(s["x3_hi"], 1)

        def group(b, t, first, nxt):
            for cc in range(4):
                cf = C * b + 4 * t + cc
                act.wait_ge(s["up_mm"], cf + 1)
                act.wait_ge(s["hid_mul"], cf)
                act.activation(sil, up_ps[:, :], ACT.Silu, scale=qs[:, 0:1]).then_inc(s["up_act"], 1)
                act.wait_ge(s["hid_mul"], cf + 1)
                if not (first and cc < 2):
                    act.wait_ge(s["down_mm"], cf - 1)
                act.activation(hid[:, cc % 2, 0], h32, ACT.Copy).then_inc(s["hid_hi"], 1)
                if nxt and cc == 2:
                    x3_hi(b + 1, t)

        for t in range(T):
            x3_hi(0, t, ps[t])

        def batch3(b, first, nxt):
            group(b, 0, first, nxt)
            with act.Fori(1, T) as t:
                group(b, t, False, nxt)

        batch3(0, True, True)
        with act.Fori(1, B - 1) as b:
            batch3(b, False, True)
        batch3(B - 1, False, False)

    @block.vector
    def _(dve):
        def tile_stats(i, t, src, stat):
            dve.bn_stats(st[i][:, t], src).then_inc(s[stat], 1)

        def aggregate(i, t, stat, n, aggr):
            wait_apart(dve, stat, n)
            dve.bn_aggr(mv[i][:, t], st[i][:, t]).then_inc(s[aggr], 1)

        def normalise(i, dst, src, t, done):
            dve.tensor_scalar(dst, src, mv[i][:, t, 0:1], rs[i][:, t:t + 1], ALU.subtract, ALU.mult).then_inc(s[done], 1)

        def x_tile(n):
            return resid[:, bass.ds(n, 1)].rearrange("p a d -> p (a d)")

        def first_stats(b1):
            for t in range(T):
                tile_stats(0, t, x_tile(T * b1 + t), "x_stat")
            for t in range(T):
                aggregate(0, t, "x_stat", T * b1 + T, "x_aggr")

        def first_norm(b1):
            dve.wait_ge(s["rs1"], 2 * b1)
            dve.wait_ge(s["t1_mm"], T * b1)
            for t in range(T):
                normalise(0, nrm[:, t], x_tile(T * b1 + t), t, "x_norm")

        def first_norm_lo(b1, tiles):
            for t in tiles:
                dve.wait_ge(s["x_hi"], T * b1 + t + 1)
                cut = slice(t * P, (t + 1) * P)
                dve.tensor_tensor(xT[:, 1, :, cut], tr[t % 2].rearrange("p (k s) -> p k s", k=K),
                                  xT[:, 0, :, cut], ALU.subtract).then_inc(s["x_lo"], 1)

        def split(m):
            dve.wait_ge(s["w_hi"], m + 1)
            dve.tensor_tensor(w_att[:, m, 1], att_slot[m], w_att[:, m, 0], ALU.subtract).then_inc(s["w_lo"], 1)

        step = [0]

        def route(ins):
            step[0] += 1
            ins.then_inc(s["route_step"], 1)
            dve.wait_ge(s["route_step"], step[0])

        def routing_members():
            dve.wait_ge(s["tok_in"], 16)
            route(dve.tensor_copy(tokf[:, :], tok[:, :]))
            dve.memset(ge[:, 0], 1.0).then_inc(s["route_step"], 1)
            dve.memset(ge[:, E], 0.0).then_inc(s["route_step"], 1)
            for e in range(1, E):
                dve.tensor_scalar(ge[:, e], tokf[:, :], float(e * (VOCAB // E)), None, ALU.is_ge).then_inc(s["route_step"], 1)
            step[0] += E + 1
            dve.wait_ge(s["route_step"], step[0])
            route(dve.tensor_tensor(member[:, :, :], ge[:, 0:E], ge[:, 1:E + 1], ALU.subtract))

        def routing_starts():
            dve.wait_ge(s["route_mm"], 2)
            route(dve.tensor_copy(scan[:, 0], kv_ps[:, 0:E * NT].rearrange("p (e c) -> p e c", e=E)))
            dve.tensor_tensor(before[:, :, :], kv_ps[:, E * NT:2 * E * NT].rearrange("p (e c) -> p e c", e=E),
                              scan[:, 0], ALU.subtract).then_inc(s["route_read"], 1)
            dve.wait_ge(s["route_read"], 1)
            a, d = 0, 1
            while d < NT:
                dve.tensor_copy(scan[:, 1 - a, :, 0:d], scan[:, a, :, 0:d]).then_inc(s["route_step"], 1)
                step[0] += 1
                route(dve.tensor_tensor(scan[:, 1 - a, :, d:NT], scan[:, a, :, d:NT], scan[:, a, :, 0:NT - d], ALU.add))
                a, d = 1 - a, 2 * d
            count = scan[:, a, :, NT - 1]
            route(dve.tensor_scalar(pad_f[:, :], count, float(P - 1), None, ALU.add))
            route(dve.tensor_copy(pad_i[:, 0], pad_f[:, :]))
            route(dve.tensor_scalar(pad_i[:, 1], pad_i[:, 0], 7, 7, ALU.logical_shift_right, ALU.logical_shift_left))
            route(dve.tensor_copy(pad_f[:, :], pad_i[:, 1]))
            route(dve.memset(base[:, :], 0.0))
            for e in range(1, E):
                route(dve.tensor_tensor(base[:, e:e + 1], base[:, e - 1:e], pad_f[:, e - 1:e], ALU.add))
            assert d == NT and a == 0

        def routing_positions():
            a = 0
            route(dve.tensor_tensor(before[:, :, :], before[:, :, :], scan[:, a], ALU.add))
            for e in range(E):
                dve.tensor_scalar(ge[:, e], before[:, e], base[:, e:e + 1], None, ALU.add).then_inc(s["route_step"], 1)
            step[0] += E
            dve.wait_ge(s["route_step"], step[0])
            route(dve.tensor_tensor(before[:, :, :], ge[:, 0:E], member[:, :, :], ALU.mult))
            route(dve.tensor_reduce(pos_f[:, :], before[:, :, :].rearrange("p e c -> p c e"), AX.X, ALU.add))
            route(dve.memset(pos[:, NT:NT + 1], 0))
            route(dve.tensor_copy(pos[:, 0:NT], pos_f[:, :]))
            dve.wait_ge(s["starts_made"], 1)
            route(dve.tensor_copy(starts[:, :], starts_i[:, :]))
            for e in range(1, E):
                dve.tensor_scalar(te_f[:, e], starts[:, :], base[0:1, e:e + 1], None, ALU.is_ge).then_inc(s["route_step"], 1)
            step[0] += E - 1
            dve.wait_ge(s["route_step"], step[0])
            route(dve.tensor_tensor(te_f[:, 0], te_f[:, 1], te_f[:, 2], ALU.add))
            route(dve.tensor_tensor(te_f[:, 1], te_f[:, 0], te_f[:, 3], ALU.add))
            dve.tensor_copy(tile_expert[:, :], te_f[:, 1]).then_inc(s["route_ready"], 1)

        def first_tile(t):
            wait_apart(dve, f"x_first{t}", 16)
            tile_stats(0, t, x_tile(t), "x_stat")
            aggregate(0, t, "x_stat", t + 1, "x_aggr")

        def first_tile_norm(t):
            dve.wait_ge(s["rs1_first"], 2 * t + 2)
            normalise(0, nrm[:, t], x_tile(t), t, "x_norm")

        first_tile(0)
        for t in range(1, T):
            first_tile(t)
            first_tile_norm(t - 1)
        first_norm_lo(0, (0, 1))
        first_tile_norm(T - 1)
        split(0)
        first_norm_lo(0, (2, 3))
        split(1)
        routing_members()
        dve.wait_ge(s["cols_in"], 64)

        def gated_mul(b, k):
            if k == 0:
                dve.wait_ge(s["zeroed"], 16 * ((SLOTS + 1) // 2))
                dve.wait_ge(s["u_act"], K * b + K)
            if k >= 2:
                dve.wait_ge(s["a_lo"], K * b + k - 1)
            dve.wait_ge(s["n_aff"], K * b + k + 1)
            dve.tensor_tensor(a32[:, k % 2], tmpA[:, k % 2], uT[:, k], ALU.mult).then_inc(s["a_mul"], 1)

        def gated_lo(b, k):
            dve.wait_ge(s["a_hi"], K * b + k + 1)
            dve.tensor_tensor(aT[:, 1, k], a32[:, k % 2], aT[:, 0, k], ALU.subtract).then_inc(s["a_lo"], 1)

        def v_bias(b, t):
            dve.wait_ge(s["v_mm"], T * b + t + 1)
            dve.tensor_tensor(vv[:, t], acc[t % 2][:, :], bv_bc[:, :], ALU.add).then_inc(s["v_bias"], 1)

        def head_norm(b):
            dve.wait_ge(s["rs_o"], 2 * b + 2)
            for t in range(T):
                normalise(1, on[:, t], on[:, t], t, "o_norm")

        def head_stats(b, t):
            wait_apart(dve, "o_copy", T * b + t + 1)
            tile_stats(1, t, on[:, t], "o_stat")

        def last_head_norm(t):
            dve.wait_ge(s["rs_o_last"], 2 * t + 2)
            normalise(1, on[:, t], on[:, t], t, "o_norm")

        def residual(b, t):
            dve.wait_ge(s["wo_mm"], T * b + t + 1)
            dve.wait_ge(s["bias_added"], T * b + t + 1)
            dve.tensor_tensor(x_tile(T * b + t), acc[t % 2][:, :], x_tile(T * b + t), ALU.add).then_inc(s["x1_done"], 1)

        def second_stats(b, t):
            wait_apart(dve, "x1_done", T * b + t + 1)
            tile_stats(2, t, x_tile(T * b + t), "x2_stat")

        def second_norm(b, t):
            normalise(2, n2[:, t], x_tile(T * b + t), t, "x2_norm")

        def copy_pos(b):
            dve.tensor_copy(pos_now[:, :], pos[:, bass.ds(T * b, T)])

        def ctx_lo(b, k):
            dve.wait_ge(s["ctx_hi"], 4 * b + k + 1)
            hi = w_moe[:, bass.ds(b, 1), 0, k].rearrange("p a d -> p (a d)")
            lo = w_moe[:, bass.ds(b, 1), 1, k].rearrange("p a d -> p (a d)")
            dve.scalar_tensor_tensor(out=lo, in0=prep[:, :], scalar=CTX_SCALE, in1=hi, op0=ALU.mult,
                                     op1=ALU.subtract).then_inc(s["ctx_lo"], 1)

        def q_elu(b, m):
            dve.wait_ge(s["q_exp"], K * b + m + 1)
            dve.tensor_scalar(tmp[:, m % 2], tmp[:, m % 2], 1.0, -1.0, ALU.min, ALU.add).then_inc(s["q_clip"], 1)
            dve.wait_ge(s["q_clip"], K * b + m + 1)
            dve.scalar_tensor_tensor(out=qT[:, m], in0=acc[m % 2][:, :], scalar=cols[:, 0, m:m + 1],
                                     in1=tmp[:, m % 2], op0=ALU.add, op1=ALU.max).then_inc(s["q_elu"], 1)

        def batch(b, first, last):
            dve.wait_ge(s["o_mm"], T * b)
            q_elu(b, 0)
            q_elu(b, 1)
            if not first:
                head_norm(b - 1)
            q_elu(b, 2)
            q_elu(b, 3)
            dve.wait_ge(s["kv_mm"], b)
            if first:
                split(2)
                dve.wait_ge(s["rows_in"], 32)
                for t in range(T):
                    v_bias(b, t)
                routing_starts()
                ctx_lo(b, 0)
                dve.wait_ge(s["x_rest"], 16)
            else:
                ctx_lo(b, 0)
                copy_pos(b - 1)
                gated_mul(b - 1, 0)
                gated_mul(b - 1, 1)
                gated_lo(b - 1, 0)
                v_bias(b, 0)
                gated_mul(b - 1, 2)
                gated_lo(b - 1, 1)
                v_bias(b, 1)
                gated_mul(b - 1, 3)
                gated_lo(b - 1, 2)
                gated_lo(b - 1, 3)
                v_bias(b, 2)
                v_bias(b, 3)
                ctx_lo(b, 1)
                for t in range(T):
                    residual(b - 1, t)
                ctx_lo(b, 2)
                for t in range(T):
                    second_stats(b - 1, t)
                for t in range(T):
                    aggregate(2, t, "x2_stat", T * b, "x2_aggr")
            if not last:
                first_stats(b + 1)
            if first:
                for k in range(1, K):
                    ctx_lo(b, k)
            else:
                ctx_lo(b, 3)
                dve.wait_ge(s["rs2"], 2 * b)
                for t in range(T):
                    second_norm(b - 1, t)
            if not last:
                first_norm(b + 1)
            if first:
                split(3)
            if not last:
                first_norm_lo(b + 1, (0, 1))
            dve.wait_ge(s["kv_mm"], b + 1)
            dve.wait_ge(s["pool_const"], 7)
            dve.tensor_tensor(kvm[:].rearrange("p k e -> p (k e)"), kv_ps[:, :],
                              head_mask[:].rearrange("p k e -> p (k e)"), ALU.mult).then_inc(s["kv_evac"], 1)
            if not last:
                first_norm_lo(b + 1, (2, 3))
            if first:
                routing_positions()
            if last:
                for t in range(T):
                    head_stats(b, t)
                    aggregate(1, t, "o_stat", T * b + t + 1, "o_aggr")
                    if t > 0:
                        last_head_norm(t - 1)
                last_head_norm(T - 1)
            else:
                for t in range(T):
                    head_stats(b, t)
                for t in range(T):
                    aggregate(1, t, "o_stat", T * b + T, "o_aggr")
            if not first:
                dve.wait_ge(s["scattered"], 16 * T * b)

        def signs_of(g, j):
            dve.wait_ge(s[f"unit_in{j}"], 16 * (g + 1))
            if not (isinstance(g, int) and g == 0):
                dve.wait_ge(s["unit_mm"], T * (3 * g + j - 2))
            dve.tensor_scalar(signs[:, j, 0], unit_slot[j], thr[:, 0, j:j + 1], None, ALU.is_gt).then_inc(s["sign_a"], 1)
            dve.tensor_scalar(signs[:, j, 1], unit_slot[j], thr[:, 1, j:j + 1], -1.0, ALU.is_lt,
                              ALU.mult).then_inc(s["sign_b"], 1)

        batch(0, True, False)
        with dve.Fori(1, B - 1) as b:
            batch(b, False, False)
        batch(B - 1, False, True)

        dve.wait_ge(s["abs_done"], 3 * B)
        dve.tensor_reduce(abssum[:, :], absacc[:, :, :], AX.X, ALU.add).then_inc(s["scale_step"], 1)
        dve.wait_ge(s["abs_mm"], 1)
        dve.tensor_scalar(qs[:, :], prep[:, 0:3], 1.0 / (FF * D), Q_EPS, ALU.mult, ALU.add).then_inc(s["scale_step"], 1)
        dve.wait_ge(s["scale_step"], 2)
        dve.tensor_scalar(thr[:, 0], qs[:, :], 0.5, None, ALU.mult).then_inc(s["scale_step"], 1)
        dve.tensor_scalar(thr[:, 1], qs[:, :], -0.5, None, ALU.mult).then_inc(s["scale_step"], 1)
        dve.tensor_tensor(hk[:, 1:2], qs[:, 0:1], qs[:, 1:2], ALU.mult).then_inc(s["scale_step"], 1)
        dve.wait_ge(s["scale_step"], 5)
        dve.tensor_scalar(hk[:, 1:2], hk[:, 1:2], qs[:, 2:3], HID_SCALE, ALU.mult, ALU.mult).then_inc(s["scale_step"], 1)
        dve.reciprocal(hk[:, 0:1], qs[:, 0:1]).then_inc(s["scale_step"], 1)
        dve.wait_ge(s["scale_step"], 7)
        dve.tensor_scalar(hk[:, 0:1], hk[:, 0:1], 1.0 / HID_SCALE, None, ALU.mult).then_inc(s["scale_step"], 1)
        dve.wait_ge(s["scale_step"], 8)
        copy_pos(B - 1)
        gated_mul(B - 1, 0)
        for k in range(1, K):
            gated_mul(B - 1, k)
            gated_lo(B - 1, k - 1)
        gated_lo(B - 1, K - 1)
        signs_of(0, 0)

        def last_sum(t):
            residual(B - 1, t)
            second_stats(B - 1, t)
            aggregate(2, t, "x2_stat", T * (B - 1) + t + 1, "x2_aggr")

        def last_norm(t):
            dve.wait_ge(s["rs2_last"], 2 * t + 2)
            second_norm(B - 1, t)

        last_sum(0)
        for t in range(1, T):
            last_sum(t)
            last_norm(t - 1)
        last_norm(T - 1)
        signs_of(0, 1)
        signs_of(0, 2)
        signs_of(1, 0)

        def xs_lo(i):
            dve.wait_ge(s["xs_hi"], i + 1)
            dve.tensor_tensor(xsT[:, 1], tx_ps[:, :], xsT[:, 0], ALU.subtract).then_inc(s["xs_lo"], 1)

        def y_copy(i, slot, uses):
            dve.wait_ge(s["y_mm"], i + 1)
            dve.wait_ge(s[f"ys_out{slot}"], 16 * uses)
            dve.tensor_scalar(ys_slot[slot], y_ps[:, :], CTX_SCALE ** -2, None, ALU.mult).then_inc(s["y_evac"], 1)

        def tile_step(i, quant, prev_slot, prev_uses):
            if quant is not None:
                signs_of(*quant)
            dve.wait_ge(s["z_act"], i + 1)
            dve.wait_ge(s["h_hi"], i)
            dve.tensor_tensor(h32, z_ps[:, :], sil, ALU.mult).then_inc(s["h_mul"], 1)
            xs_lo(i + 1)
            if prev_slot is not None:
                y_copy(i - 1, prev_slot, prev_uses)
            dve.wait_ge(s["h_hi"], i + 1)
            dve.tensor_tensor(hT[:, 1], th_ps[:, :], hT[:, 0], ALU.subtract).then_inc(s["h_lo"], 1)

        xs_lo(0)
        signs_of(1, 1)
        tile_step(0, (1, 2), None, None)
        for j in range(3):
            tile_step(j + 1, (2, j), j, 0)
        with dve.Fori(1, 6) as g:
            for j in range(3):
                tile_step(3 * g + j + 1, None, j, g)
        dve.wait_ge(s["scattered"], 16 * NT)
        dve.tensor_copy(pos_now[:, :], pos[:, 0:T]).then_inc(s["pos3_copied"], 1)
        signs_of(3, 0)
        y_copy(SLOTS - 1, 0, 6)
        signs_of(3, 1)
        signs_of(3, 2)

        def x3_lo(b, t, bank=t3_ps):
            dve.wait_ge(s["x3_hi"], T * b + t + 1)
            cut = bass.ds(t * P, P)
            hi = x3T[:, bass.ds(b, 1), 0, :, cut].rearrange("p a k s -> p (a k) s")
            lo = x3T[:, bass.ds(b, 1), 1, :, cut].rearrange("p a k s -> p (a k) s")
            dve.tensor_tensor(lo, bank[:, :].rearrange("p (k s) -> p k s", k=K), hi, ALU.subtract).then_inc(s["x3_lo"], 1)

        def sum3(t):
            dve.wait_ge(s[f"y_in_first{t}"], 16)
            dve.tensor_tensor(x_tile(t), n2[:, t], x_tile(t), ALU.add).then_inc(s["y_added"], 1)

        def stats3(t):
            wait_apart(dve, "y_added", t + 1)
            tile_stats(0, t, x_tile(t), "x3_stat")

        def aggregate3(t):
            aggregate(0, t, "x3_stat", t + 1, "x3_aggr")

        def norm3(t):
            dve.wait_ge(s["rs3_first"], 2 * t + 2)
            normalise(0, nrm[:, t], x_tile(t), t, "x3_norm")

        sum3(0)
        sum3(1)
        stats3(0)
        sum3(2)
        stats3(1)
        aggregate3(0)
        sum3(3)
        stats3(2)
        aggregate3(1)
        norm3(0)
        stats3(3)
        aggregate3(2)
        norm3(1)
        aggregate3(3)
        norm3(2)
        norm3(3)
        dve.tensor_copy(pos_now[:, 0:1], pos[:, T:T + 1]).then_inc(s["pos3_copied"], 1)
        for t in range(T):
            x3_lo(0, t, ps[t])

        def x3_sum(b, t):
            i = T * b + t
            dve.wait_ge(s["y_in"], (i - T) * 16 + 16)
            dve.tensor_tensor(x_tile(i), n2[:, 0], x_tile(i), ALU.add).then_inc(s["y_added"], 1)
            wait_apart(dve, "y_added", i + 1)
            dve.bn_stats(st[0][:, 0], x_tile(i)).then_inc(s["x3_stat"], 1)
            wait_apart(dve, "x3_stat", i + 1)
            dve.bn_aggr(mv[0][:, 0], st[0][:, 0]).then_inc(s["x3_aggr"], 1)

        def x3_normalise(b, t):
            i = T * b + t
            dve.wait_ge(s["rs3"], 2 * (i - T) + 2)
            dve.wait_ge(s["t3_mm"], i)
            normalise(0, nrm[:, 0], x_tile(i), 0, "x3_norm")

        def next_pos(i):
            dve.tensor_copy(pos_now[:, 0:1], pos[:, bass.ds(i, 1)]).then_inc(s["pos3_copied"], 1)

        def finish(b, last):
            if not last:
                dve.wait_ge(s["down_mm"], C * b + C)
            for t in range(T):
                if last:
                    dve.wait_ge(s["down_last"], t + 1)
                dve.scalar_tensor_tensor(out=out_slot[t], in0=ffy_ps[t][:, :], scalar=hk[:, 1:2],
                                         in1=x_tile(T * b + t), op0=ALU.mult, op1=ALU.add).then_inc(s["out_made"], 1)

        def group(b, t, begins, first, nxt):
            for cc in range(4):
                cf = C * b + 4 * t + cc
                if begins and cc == 1 and not first:
                    finish(b - 1, False)
                if nxt and cc == 0:
                    x3_sum(b + 1, t)
                    next_pos(T * (b + 1) + t + 1)
                if nxt and cc == 1:
                    x3_normalise(b + 1, t)
                dve.wait_ge(s["up_act"], cf + 1)
                dve.wait_ge(s["gate_mm"], cf + 1)
                dve.wait_ge(s["hid_hi"], cf)
                dve.wait_ge(s["hid_lo"], cf)
                dve.scalar_tensor_tensor(out=h32, in0=sil, scalar=hk[:, 0:1], in1=gate_ps[:, :], op0=ALU.mult,
                                         op1=ALU.mult).then_inc(s["hid_mul"], 1)
                dve.wait_ge(s["hid_hi"], cf + 1)
                dve.tensor_tensor(hid[:, cc % 2, 1], h32, hid[:, cc % 2, 0], ALU.subtract).then_inc(s["hid_lo"], 1)
                if nxt and cc == 2:
                    x3_lo(b + 1, t)

        def batch3(b, first, nxt):
            group(b, 0, True, first, nxt)
            with dve.Fori(1, T) as t:
                group(b, t, False, False, nxt)
            if not first:
                for t in range(T):
                    dve.wait_ge(s[f"out_done{t}"], 16 * b)

        batch3(0, True, True)
        with dve.Fori(1, B - 1) as b:
            batch3(b, False, True)
        batch3(B - 1, False, False)
        finish(B - 1, True)

    @block.tensor
    def _(pe):
        def transposes(dst, src):
            for i in range(4):
                mm = pe.transpose(dst[:, i * P:(i + 1) * P], src(i), ident[:, :])
            return mm

        def partial(dst, lhs, rhs, pairs, chunks, start, stop):
            steps = [(i, j, k) for k in chunks for i, j in pairs]
            for n, step in enumerate(steps):
                mm = pe.matmul(dst, lhs(*step), rhs(*step), start=(start and n == 0), stop=(stop and n == len(steps) - 1))
            return mm

        def product(dst, lhs, rhs):
            return partial(dst, lhs, rhs, PARTS, range(K), True, True)

        def first_norm(b1, tiles):
            for t in tiles:
                pe.wait_ge(s["x_norm"], T * b1 + t + 1)
                if t >= 2:
                    pe.wait_ge(s["x_lo"], T * b1 + t - 1)
                elif not (isinstance(b1, int) and b1 == 0):
                    pe.wait_ge(s["k_copy"], T * b1 - 1 + t)
                transposes(tr[t % 2], lambda k: nrm[:, t, k * P:(k + 1) * P]).then_inc(s["t1_mm"], 1)

        def ctx_part(b, k):
            pe.wait_ge(s["ctx_lo"], 4 * b + k)
            transposes(prep, lambda r: stage[:, 0, r, k * P:(k + 1) * P]).then_inc(s["ctx_mm"], 1)

        def head_norm(b, last, chunks):
            pe.wait_ge(s["o_norm"], T * b + T)
            for k in chunks:
                if k < 2:
                    if last:
                        pe.wait_ge(s["k_copy"], T * b + 3 + k)
                    else:
                        pe.wait_ge(s["x_lo"], T * (b + 1) + 3 + k)
                else:
                    pe.wait_ge(s["n_aff"], K * b + k - 1)
                transposes(tr[k % 2], lambda t: on[:, t, k * P:(k + 1) * P]).then_inc(s["tn_mm"], 1)

        def project(b, bank_free):
            pe.wait_ge(s["w_lo"], 4)
            if bank_free is not None:
                pe.wait_ge(s["a_lo"], K * b + K)
            for t in range(T):
                if t < 2:
                    if bank_free is not None:
                        pe.wait_ge(s["v_bias"], bank_free + t)
                else:
                    pe.wait_ge(s["x1_done"], T * b + t - 1)
                cut = slice(t * P, (t + 1) * P)
                dst = acc[t % 2][:, :]
                lhs, rhs = lambda i, j, k: aT[:, i, k, cut], lambda i, j, k: w_att[:, 3, j, k]
                if bank_free is None and t == 0:
                    for k in range(K):
                        pe.wait_ge(s["a_lo"], K * b + k + 1)
                        mm = partial(dst, lhs, rhs, PARTS, [k], k == 0, k == K - 1)
                    mm.then_inc(s["wo_mm"], 1)
                else:
                    product(dst, lhs, rhs).then_inc(s["wo_mm"], 1)

        def batch(b, first, last):
            if not first:
                pe.wait_ge(s["x_lo"], T * b + T)
            for m in range(K):
                if m < 2:
                    if not first:
                        pe.wait_ge(s["u_act"], K * (b - 1) + 3 + m)
                else:
                    pe.wait_ge(s["q_elu"], K * b + m - 1)
                dst = acc[m % 2][:, :]
                lhs, rhs = lambda i, j, k: w_att[:, 0, j, k, m * P:(m + 1) * P], lambda i, j, k: xT[:, i, k]
                if first and m == 0:
                    pe.wait_ge(s["w_hi"], 1)
                    pe.wait_ge(s["x_hi"], T)
                    partial(dst, lhs, rhs, [(0, 0)], range(K), True, False)
                    pe.wait_ge(s["w_lo"], 1)
                    partial(dst, lhs, rhs, [(0, 1)], range(K), False, False)
                    pe.wait_ge(s["x_lo"], T)
                    partial(dst, lhs, rhs, [(1, 0)], range(K), False, True).then_inc(s["q_mm"], 1)
                else:
                    product(dst, lhs, rhs).then_inc(s["q_mm"], 1)
                if not first and m == 1:
                    pe.wait_ge(s["stage_in0"], 32 * b + 16)
                    ctx_part(b, 0)
            if first:
                routing_sums()
            else:
                head_norm(b - 1, False, (0, 1))
            pe.wait_ge(s["w_lo"], 2)
            for t in range(T):
                if t < 2:
                    pe.wait_ge(s["q_elu"], K * b + 3 + t)
                else:
                    pe.wait_ge(s["v_bias"], T * b + t - 1)
                cut = slice(t * P, (t + 1) * P)
                product(acc[t % 2][:, :], lambda i, j, k: xT[:, i, k, cut],
                        lambda i, j, k: w_att[:, 1, j, k]).then_inc(s["v_mm"], 1)
                if not first and t == 0:
                    head_norm(b - 1, False, (2, 3))
            if not first:
                ctx_part(b, 1)
                project(b - 1, T * b + 3)
            for t in range(T):
                if t < 2:
                    if first:
                        pe.wait_ge(s["x_lo"], 3 + t)
                    else:
                        pe.wait_ge(s["n_aff"], K * (b - 1) + 3 + t)
                else:
                    pe.wait_ge(s["k_copy"], T * b + t - 1)
                transposes(tr[t % 2], lambda k: qT[:, k, t * P:(t + 1) * P]).then_inc(s["tk_mm"], 1)
                if not first and t == 1:
                    ctx_part(b, 2)
            if first:
                pe.wait_ge(s["stage_in0"], 16)
                ctx_part(b, 0)
            pe.wait_ge(s["w_lo"], 3)
            for m in range(K):
                if m < 2:
                    if first:
                        pe.wait_ge(s["v_bias"], 3 + m)
                    else:
                        pe.wait_ge(s["x1_done"], T * (b - 1) + 3 + m)
                else:
                    pe.wait_ge(s["u_act"], K * b + m - 1)
                product(acc[m % 2][:, :], lambda i, j, k: w_att[:, 2, j, k, m * P:(m + 1) * P],
                        lambda i, j, k: xT[:, i, k]).then_inc(s["u_mm"], 1)
                if first and m < 3:
                    ctx_part(b, m + 1)
                elif not first and m == 0:
                    ctx_part(b, 3)
            if not last:
                first_norm(b + 1, (0, 1))
            pe.wait_ge(s["k_copy"], T * b + T)
            pe.wait_ge(s["v_act"], T * b + T)
            pe.wait_ge(s["kv_evac"], b)
            if first:
                pe.wait_ge(s["route_read"], 1)
            for m in range(K):
                cut = slice(m * P, (m + 1) * P)
                for t in range(T):
                    mm = pe.matmul(kv_ps[:, cut], kk[:, t, cut], vv[:, t, cut], start=(t == 0), stop=(t == T - 1))
            mm.then_inc(s["kv_mm"], 1)
            if not last:
                first_norm(b + 1, (2, 3))
            pe.wait_ge(s["kv_evac"], b + 1)
            for t in range(T):
                if t < 2:
                    if not first:
                        pe.wait_ge(s["o_copy"], T * (b - 1) + 3 + t)
                else:
                    pe.wait_ge(s["o_copy"], T * b + t - 1)
                for k in range(K):
                    cut = slice(k * P, (k + 1) * P)
                    mm = pe.matmul(o_ps[t % 2][:, cut], qT[:, k, t * P:(t + 1) * P], kvm[:, k], start=True, stop=True)
                mm.then_inc(s["o_mm"], 1)

        def routing_sums():
            pe.wait_ge(s["route_step"], E + 3)
            pe.wait_ge(s["pool_const"], 3)
            flat = member[:, :, :].rearrange("p e c -> p (e c)")
            n = E * NT
            pe.matmul(kv_ps[:, 0:n], ones[:, :], flat, start=True, stop=True).then_inc(s["route_mm"], 1)
            pe.matmul(kv_ps[:, n:2 * n], tri[:, :], flat, start=True, stop=True).then_inc(s["route_mm"], 1)

        def unit_transposes(g, j):
            pe.wait_ge(s["sign_b"], 3 * g + j + 1)
            for r in range(T):
                if not (isinstance(g, int) and g == 0 and j == 0):
                    pe.wait_ge(s["unit_copy"], T * (3 * g + j - 1) + r + 1)
                for q in range(T):
                    cut = slice(q * P, (q + 1) * P)
                    for h in range(2):
                        mm = pe.matmul(q_ps[r][:, cut], signs[:, j, h, r, cut], ident_b[:, :],
                                         start=(h == 0), stop=(h == 1))
                mm.then_inc(s["unit_mm"], 1)

        pe.wait_ge(s["ident_made"], 1)
        first_norm(0, range(T))
        batch(0, True, False)
        with pe.Fori(1, B - 1) as b:
            batch(b, False, False)
        batch(B - 1, False, True)
        pe.wait_ge(s["scale_step"], 1)
        pe.wait_ge(s["ctx_lo"], 4 * B)
        pe.matmul(prep[:, 0:3], ones[:, :], abssum[:, :], start=True, stop=True).then_inc(s["abs_mm"], 1)
        head_norm(B - 1, True, range(K))
        project(B - 1, None)
        pe.wait_ge(s["scale_step"], 2)
        pe.wait_ge(s["o_copy"], NT)
        for j in range(3):
            unit_transposes(0, j)

        def xs_transpose(i, slot, slot_count):
            pe.wait_ge(s[f"xs_in{slot}"], 16 * slot_count)
            pe.wait_ge(s["xs_lo"], i)
            transposes(tx_ps, lambda k: xs_slot[slot][:, k * P:(k + 1) * P]).then_inc(s["tx_mm"], 1)

        def expert(i):
            return pe.value_load(tile_expert[0:1, bass.ds(i, 1)], min_val=0, max_val=E - 1)

        def moe(dst, lhs, e):
            return product(dst, lambda i, j, k: lhs[:, i, k * P:(k + 1) * P],
                           lambda i, j, k: w_moe[:, bass.ds(e, 1), j, k].rearrange("p a d -> p (a d)"))

        def second(i):
            e = expert(i)
            pe.wait_ge(s["h_lo"], i + 1)
            pe.wait_ge(s["y_evac"], i)
            moe(y_ps[:, :], hT, e).then_inc(s["y_mm"], 1)

        def tile_step(i, units, slot, slot_count, first):
            e = expert(i)
            pe.wait_ge(s["xs_lo"], i + 1)
            pe.wait_ge(s["h_mul"], i)
            moe(z_ps[:, :], xsT, e).then_inc(s["z_mm"], 1)
            xs_transpose(i + 1, slot, slot_count)
            if not first:
                second(i - 1)
            for g, j in units:
                unit_transposes(g, j)
            pe.wait_ge(s["h_mul"], i + 1)
            pe.wait_ge(s["h_lo"], i)
            transposes(th_ps, lambda k: h32[:, k * P:(k + 1) * P]).then_inc(s["th_mm"], 1)

        pe.wait_ge(s["route_ready"], 1)
        xs_transpose(0, 0, 1)
        unit_transposes(1, 0)
        tile_step(0, ((1, 1), (1, 2)), 1, 1, True)
        for j in range(3):
            tile_step(j + 1, ((2, j),), (j + 2) % 3, 1 + (j + 2) // 3, False)
        with pe.Fori(1, 6) as g:
            for j in range(3):
                tile_step(3 * g + j + 1, (), (j + 2) % 3, g + 1 + (j + 2) // 3, False)
        second(SLOTS - 1)
        for j in range(3):
            unit_transposes(3, j)

        def x3_transpose(i, t, bank):
            pe.wait_ge(s["x3_norm"], i + 1)
            if bank is t3_ps:
                pe.wait_ge(s["x3_lo"], i)
            transposes(bank, lambda k: nrm[:, t, k * P:(k + 1) * P]).then_inc(s["t3_mm"], 1)

        def two_pass(dst, w, cf_c, b, first=False):
            for i in range(2):
                if first:
                    pe.wait_ge(s["x3_lo" if i else "x3_hi"], T)
                for k in range(K):
                    mm = pe.matmul(dst, w[:, bass.ds(cf_c, 1), k * P:(k + 1) * P].rearrange("p a n -> p (a n)"),
                                     x3T[:, bass.ds(b, 1), i, k].rearrange("p a s -> p (a s)"),
                                     start=(i == 0 and k == 0), stop=(i == 1 and k == K - 1))
            return mm

        def down(cf, c, parity, start, stop):
            pe.wait_ge(s["hid_lo"], cf + 1)
            for t in range(T):
                for i in range(2):
                    mm = pe.matmul(ffy_ps[t][:, :], hid[:, parity, i, t * P:(t + 1) * P],
                                     tern[2][:, bass.ds(c, 1)].rearrange("p a n -> p (a n)"),
                                     start=(start and i == 0), stop=(stop and i == 1))
            mm.then_inc(s["down_mm"], 1)

        def group(b, t, begins, first, nxt):
            for cc in range(4):
                c = 4 * t + cc
                cf = C * b + c
                begin = first and cc == 0
                if not begin:
                    pe.wait_ge(s["up_act"], cf)
                two_pass(up_ps[:, :], tern[0], c, b, begin).then_inc(s["up_mm"], 1)
                if not begin:
                    pe.wait_ge(s["hid_mul"], cf)
                two_pass(gate_ps[:, :], tern[1], c, b).then_inc(s["gate_mm"], 1)
                if begins and cc == 0:
                    if not first:
                        down(cf - 1, C - 1, 1, False, True)
                else:
                    if begins and cc == 1 and not first:
                        pe.wait_ge(s["out_made"], T * b)
                    down(cf - 1, c - 1, (cc - 1) % 2, begins and cc == 1, False)
                if nxt and cc == 1:
                    x3_transpose((b + 1) * T + t, 0, t3_ps)

        for t in range(T):
            x3_transpose(t, t, ps[t])
        pe.wait_ge(s["unit_copy"], 12 * T)

        def batch3(b, first, nxt):
            if not first:
                pe.wait_ge(s["x3_lo"], T * b + T)
            group(b, 0, True, first, nxt)
            with pe.Fori(1, T) as t:
                group(b, t, False, False, nxt)

        batch3(0, True, True)
        with pe.Fori(1, B - 1) as b:
            batch3(b, False, True)
        batch3(B - 1, False, False)
        for i in range(2):
            pe.wait_ge(s["hid_lo" if i else "hid_hi"], C * B)
            for t in range(T):
                mm = pe.matmul(ffy_ps[t][:, :], hid[:, 1, i, t * P:(t + 1) * P], tern[2][:, C - 1],
                               start=False, stop=(i == 1))
                if i == 1:
                    mm.then_inc(s["down_last"], 1)

    es.close()


_INS = ['x', 'itok_BxS_13_99985', 'ctx_2048', 'L0_attn_Wqk', 'L0_attn_bqk', 'L0_attn_Wv', 'L0_attn_bv', 'L0_attn_Wu',
        'L0_attn_bu', 'L0_attn_Wo', 'L0_attn_bo', 'L0_attn_ln_g', 'L0_attn_ln_b', 'L0_ffn_W_up', 'L0_ffn_W_gate',
        'L0_ffn_W_down']


def kernel(**inputs):
    import concourse.bacc as _bacc
    from concourse.bass_utils import run_bass_kernel_spmd as _run

    nc = _bacc.Bacc("TRN2", target_bir_lowering=False, num_devices=1)
    arrays, args = {}, []
    for name in _INS:
        a = np.ascontiguousarray(inputs[name])
        arrays[f"in_{name}_dram"] = a
        args.append(nc.dram_tensor(f"in_{name}_dram", a.shape, mybir.dt.from_np(a.dtype), kind="ExternalInput").ap())
    args.append(nc.dram_tensor("out_0_dram", (B, S, D), F32, kind="ExternalOutput").ap())
    decoder(nc, *args)
    r = _run(nc, [arrays], core_ids=[0])
    return r.results[0]["out_0_dram"]
```
